# Optimizing a Trainium2 kernel written in Bass

```python
import numpy as np
import jax
import jax.numpy as jnp

def _softmax(x, axis=-1):
    return jax.nn.softmax(x, axis=axis)

def _gelu(x):
    return jax.nn.gelu(x, approximate=True)

def _silu(x):
    return jax.nn.silu(x)

def _sigmoid(x):
    return jax.nn.sigmoid(x)

def _layernorm(x, axis=-1, eps=1e-05):
    m = jnp.mean(x, axis=axis, keepdims=True)
    v = jnp.var(x, axis=axis, keepdims=True)
    return (x - m) / jnp.sqrt(v + eps)

def _scatter_add(tgt, idx, src, axis=0):
    return tgt.at[idx].add(src)

def _segment_sum(src, seg, n):
    return jax.ops.segment_sum(src, seg, n)
kernel_name = 'mk_gnn_resnorm_d4_gnn_r16_e3bad9'

def setup_inputs(seed: int=0):
    np.random.seed(seed)
    _w = jnp.asarray

    def _rec_inputs():
        import jax
        import jax.numpy as jnp
        _gk = jax.random.key(seed)
        x = -0.0002117 + 1 * jax.random.normal(jax.random.fold_in(_gk, 1), (3125, 256), jnp.float32)
        src = jax.random.randint(jax.random.fold_in(_gk, 2), (100000,), 0, 3125, jnp.int32)
        dst = jax.random.randint(jax.random.fold_in(_gk, 3), (100000,), 0, 3125, jnp.int32)
        _o = jnp.argsort(dst, stable=True)
        src = src[_o]
        dst = dst[_o]
        edge_type_8 = jax.random.randint(jax.random.fold_in(_gk, 13), (100000,), 0, 8, jnp.int32)
        edge_weight = jax.random.uniform(jax.random.fold_in(_gk, 14), (100000,), jnp.float32, 0.0, 0.999998)
        edge_weight_n2 = jax.random.uniform(jax.random.fold_in(_gk, 15), (100000,), jnp.float32, 0.0, 0.999998)
        return (x, src, dst, edge_type_8, edge_weight, edge_weight_n2)
    x, src, dst, edge_type_8, edge_weight, edge_weight_n2 = _rec_inputs()

    def _L0_gnn_setup():
        import jax, jax.numpy as jnp
        import numpy as np
        N_NODES = 6250
        N_EDGES = 50000
        DIM = 256
        EPS = 1e-05
        key = jax.random.key(seed)
        ks = jax.random.split(key, 12)
        H = DIM
        s = 1.0 / np.sqrt(H)
        s2 = 1.0 / np.sqrt(2 * H)
        return {'feat': jax.random.normal(ks[0], (N_NODES, DIM), dtype=jnp.float32), 'src': jax.random.randint(ks[1], (N_EDGES,), 0, N_NODES, dtype=jnp.int32), 'dst': jax.random.randint(ks[2], (N_EDGES,), 0, N_NODES, dtype=jnp.int32), 'iw': jax.random.uniform(ks[3], (N_EDGES,), dtype=jnp.float32), 'ow': jax.random.uniform(ks[4], (N_EDGES,), dtype=jnp.float32), 'gamma': jnp.ones((DIM,), jnp.float32), 'beta': jnp.zeros((DIM,), jnp.float32), 'W_in': jax.random.uniform(ks[5], (H, H), jnp.float32, -s, s), 'b_in': jax.random.uniform(ks[6], (H,), jnp.float32, -s, s), 'W_out': jax.random.uniform(ks[7], (H, H), jnp.float32, -s, s), 'b_out': jax.random.uniform(ks[8], (H,), jnp.float32, -s, s), 'W_x2i': jax.random.uniform(ks[9], (2 * H, 2 * H), jnp.float32, -s2, s2), 'b_x2i': jax.random.uniform(ks[10], (2 * H,), jnp.float32, -s2, s2), 'W_h2h': jax.random.uniform(ks[11], (H, 2 * H), jnp.float32, -s, s)}
    _L0_gnn_all = _L0_gnn_setup()
    _L0_gnn_in = {k: v for k, v in _L0_gnn_all.items() if k in ('gamma', 'beta', 'W_in', 'b_in', 'W_out', 'b_out', 'W_x2i', 'b_x2i', 'W_h2h')}
    del _L0_gnn_all

    def _L1_gnn_setup():
        import jax, jax.numpy as jnp
        import numpy as np
        N_NODES = 1250
        N_EDGES = 20000
        IN_DIM = 256
        OUT_DIM = 256
        NUM_RELS = 8
        NUM_BASES = 4
        key = jax.random.key(seed)
        k = jax.random.split(key, 7)
        return {'h': jax.random.normal(k[0], (N_NODES, IN_DIM), dtype=jnp.float32), 'basis': jax.random.normal(k[1], (NUM_BASES, IN_DIM, OUT_DIM), dtype=jnp.float32) * (6.0 / (IN_DIM + OUT_DIM)) ** 0.5, 'w_comp': jax.random.normal(k[2], (NUM_RELS, NUM_BASES), dtype=jnp.float32), 'bias': jax.random.normal(k[3], (OUT_DIM,), dtype=jnp.float32) * 0.01, 'src': jax.random.randint(k[4], (N_EDGES,), 0, N_NODES, dtype=jnp.int32), 'dst': jax.random.randint(k[5], (N_EDGES,), 0, N_NODES, dtype=jnp.int32), 'etype': jax.random.randint(k[6], (N_EDGES,), 0, NUM_RELS, dtype=jnp.int32)}
    _L1_gnn_all = _L1_gnn_setup()
    _L1_gnn_in = {k: v for k, v in _L1_gnn_all.items() if k in ('basis', 'w_comp', 'bias')}
    del _L1_gnn_all

    def _L2_gnn_setup():
        import jax, jax.numpy as jnp
        import numpy as np
        C = 1.0
        SQC = 1.0
        MIN_NORM = 1e-15
        PROJ_EPS = 0.004

        def _norm(x):
            return jnp.clip(jnp.linalg.norm(x, axis=-1, keepdims=True), MIN_NORM)

        def logmap0(x):
            n = _norm(x)
            return jnp.arctanh(jnp.minimum(SQC * n, 1.0 - 1e-07)) * x / (SQC * n)

        def expmap0(u):
            n = _norm(u)
            return jnp.tanh(SQC * n) * u / (SQC * n)

        def proj(x):
            n = _norm(x)
            maxn = (1.0 - PROJ_EPS) / SQC
            return jnp.where(n > maxn, x / n * maxn, x)

        def mobius_add(x, y):
            x2 = jnp.sum(x * x, -1, keepdims=True)
            y2 = jnp.sum(y * y, -1, keepdims=True)
            xy = jnp.sum(x * y, -1, keepdims=True)
            num = (1.0 + 2.0 * C * xy + C * y2) * x + (1.0 - C * x2) * y
            den = 1.0 + 2.0 * C * xy + C * C * x2 * y2
            return num / jnp.clip(den, MIN_NORM)
        N, E, DIN, H, DH = (3125, 50000, 256, 4, 64)
        key = jax.random.key(seed)
        k1, k2, k3, k4, k5, k6, k7 = jax.random.split(key, 7)
        x = proj(0.01 * jax.random.normal(k1, (N, DIN), jnp.float32))
        src = jax.random.randint(k2, (E,), 0, N)
        off = jax.random.randint(k3, (E,), 1, N)
        dst = (src + off) % N
        edge_index = jnp.stack([src, dst]).astype(jnp.int64)
        glorot = float(np.sqrt(2.0 / (DIN + H * DH)))
        W = glorot * jax.random.normal(k4, (H * DH, DIN), jnp.float32)
        b_lin = 0.01 * jax.random.normal(k5, (H * DH,), jnp.float32)
        ga = float(np.sqrt(6.0 / (1 + 2 * DH)))
        att = jax.random.uniform(k6, (H, 2 * DH), jnp.float32, -ga, ga)
        b_conv = jnp.zeros((H * DH,), jnp.float32)
        return {'x': x, 'edge_index': edge_index, 'W': W, 'b_lin': b_lin, 'att': att, 'b_conv': b_conv}
    _L2_gnn_all = _L2_gnn_setup()
    _L2_gnn_in = {k: v for k, v in _L2_gnn_all.items() if k in ('W', 'b_lin', 'att', 'b_conv')}
    del _L2_gnn_all

    def _L3_gnn_setup():
        import jax, jax.numpy as jnp
        import numpy as np
        N_NODES = 3125
        N_EDGES = 50000
        D_IN = 256
        D_OUT = 256
        N_REL = 8
        key = jax.random.key(seed)
        k_x, k_ei, k_et, k_w = jax.random.split(key, 4)
        x = jax.random.normal(k_x, (N_NODES, D_IN), dtype=jnp.float32)
        edge_index = jax.random.randint(k_ei, (2, N_EDGES), 0, N_NODES, dtype=jnp.int32)
        edge_type = jax.random.randint(k_et, (N_EDGES,), 0, N_REL, dtype=jnp.int32)
        limit = float(np.sqrt(6.0 / (D_IN + D_OUT)))
        weight = jax.random.uniform(k_w, (N_REL, D_IN, D_OUT), dtype=jnp.float32, minval=-limit, maxval=limit)
        bias = jnp.zeros((D_OUT,), dtype=jnp.float32)
        return {'x': x, 'edge_index': edge_index, 'edge_type': edge_type, 'weight': weight, 'bias': bias}
    _L3_gnn_all = _L3_gnn_setup()
    _L3_gnn_in = {k: v for k, v in _L3_gnn_all.items() if k in ('weight', 'bias')}
    del _L3_gnn_all
    return {'x': x, 'src': src, 'dst': dst, 'edge_type_8': edge_type_8, 'edge_weight': edge_weight, 'edge_weight_n2': edge_weight_n2, 'L0_gnn_gamma': _L0_gnn_in['gamma'], 'L0_gnn_beta': _L0_gnn_in['beta'], 'L0_gnn_W_in': _L0_gnn_in['W_in'], 'L0_gnn_b_in': _L0_gnn_in['b_in'], 'L0_gnn_W_out': _L0_gnn_in['W_out'], 'L0_gnn_b_out': _L0_gnn_in['b_out'], 'L0_gnn_W_x2i': _L0_gnn_in['W_x2i'], 'L0_gnn_b_x2i': _L0_gnn_in['b_x2i'], 'L0_gnn_W_h2h': _L0_gnn_in['W_h2h'], 'L1_gnn_basis': _L1_gnn_in['basis'], 'L1_gnn_w_comp': _L1_gnn_in['w_comp'], 'L1_gnn_bias': _L1_gnn_in['bias'], 'L2_gnn_W': _L2_gnn_in['W'], 'L2_gnn_b_lin': _L2_gnn_in['b_lin'], 'L2_gnn_att': _L2_gnn_in['att'], 'L2_gnn_b_conv': _L2_gnn_in['b_conv'], 'L3_gnn_weight': _L3_gnn_in['weight'], 'L3_gnn_bias': _L3_gnn_in['bias']}

def reference(x, src, dst, edge_type_8, edge_weight, edge_weight_n2, L0_gnn_gamma, L0_gnn_beta, L0_gnn_W_in, L0_gnn_b_in, L0_gnn_W_out, L0_gnn_b_out, L0_gnn_W_x2i, L0_gnn_b_x2i, L0_gnn_W_h2h, L1_gnn_basis, L1_gnn_w_comp, L1_gnn_bias, L2_gnn_W, L2_gnn_b_lin, L2_gnn_att, L2_gnn_b_conv, L3_gnn_weight, L3_gnn_bias):
    import jax
    import jax.numpy as jnp

    def _L0_gnn_ref(feat, src, dst, iw, ow, gamma, beta, W_in, b_in, W_out, b_out, W_x2i, b_x2i, W_h2h):
        import jax, jax.numpy as jnp
        import numpy as np
        N_NODES = 6250
        N_EDGES = 50000
        DIM = 256
        EPS = 1e-05
        N = feat.shape[0]
        num_steps = 1
        mean = jnp.mean(feat, axis=0)
        var = jnp.var(feat, axis=0)
        h = (feat - mean) * jax.lax.rsqrt(var + EPS) * gamma + beta
        for _ in range(num_steps):
            feat_in = h @ W_in + b_in
            feat_out = h @ W_out + b_out
            a_in = jax.ops.segment_sum(feat_in[src] * iw[:, None], dst, num_segments=N)
            a_out = jax.ops.segment_sum(feat_out[dst] * ow[:, None], src, num_segments=N)
            a = jnp.concatenate((a_in, a_out), axis=1)
            xi = a @ W_x2i + b_x2i
            hh = h @ W_h2h
            i_i, i_n = jnp.split(xi, 2, axis=1)
            h_i, h_n = jnp.split(hh, 2, axis=1)
            input_gate = jax.nn.sigmoid(i_i + h_i)
            new_gate = jnp.tanh(i_n + h_n)
            h = new_gate + input_gate * (h - new_gate)
        return h

    def _L1_gnn_ref(h, basis, w_comp, bias, src, dst, etype):
        import jax, jax.numpy as jnp
        import numpy as np
        N_NODES = 1250
        N_EDGES = 20000
        IN_DIM = 256
        OUT_DIM = 256
        NUM_RELS = 8
        NUM_BASES = 4
        in_dim, out_dim = (h.shape[1], basis.shape[2])
        num_rels = w_comp.shape[0]
        wr = basis.reshape(in_dim, NUM_BASES, out_dim)
        weight = jnp.einsum('rb,ibo->iro', w_comp, wr)
        weight = weight.reshape(num_rels, in_dim, out_dim)
        t = jnp.einsum('nd,rdo->rno', h, weight)
        msg = t[etype, src]
        agg = jax.ops.segment_sum(msg, dst, num_segments=h.shape[0])
        return jax.nn.relu(agg + bias)

    def _L2_gnn_ref(x, edge_index, W, b_lin, att, b_conv):
        import jax, jax.numpy as jnp
        import numpy as np
        C = 1.0
        SQC = 1.0
        MIN_NORM = 1e-15
        PROJ_EPS = 0.004

        def _norm(x):
            return jnp.clip(jnp.linalg.norm(x, axis=-1, keepdims=True), MIN_NORM)

        def logmap0(x):
            n = _norm(x)
            return jnp.arctanh(jnp.minimum(SQC * n, 1.0 - 1e-07)) * x / (SQC * n)

        def expmap0(u):
            n = _norm(u)
            return jnp.tanh(SQC * n) * u / (SQC * n)

        def proj(x):
            n = _norm(x)
            maxn = (1.0 - PROJ_EPS) / SQC
            return jnp.where(n > maxn, x / n * maxn, x)

        def mobius_add(x, y):
            x2 = jnp.sum(x * x, -1, keepdims=True)
            y2 = jnp.sum(y * y, -1, keepdims=True)
            xy = jnp.sum(x * y, -1, keepdims=True)
            num = (1.0 + 2.0 * C * xy + C * y2) * x + (1.0 - C * x2) * y
            den = 1.0 + 2.0 * C * xy + C * C * x2 * y2
            return num / jnp.clip(den, MIN_NORM)
        N, E, DIN, H, DH = (3125, 50000, 256, 4, 64)
        n = x.shape[0]
        xh = proj(expmap0(logmap0(x) @ W.T))
        hb = proj(expmap0(b_lin[None, :]))
        xh = proj(mobius_add(xh, hb))
        loop = jnp.arange(n)
        src = jnp.concatenate([edge_index[0], loop])
        dst = jnp.concatenate([edge_index[1], loop])
        logx = logmap0(xh).reshape(H, n, DH)
        s_i = jnp.einsum('hnd,hd->nh', logx, att[:, :DH])
        s_j = jnp.einsum('hnd,hd->nh', logx, att[:, DH:])
        alpha = jax.nn.leaky_relu(s_i[dst] + s_j[src], 0.2)
        m = jax.ops.segment_max(alpha, dst, num_segments=n)
        a = jnp.exp(alpha - m[dst])
        ssum = jax.ops.segment_sum(a, dst, num_segments=n)
        a = a / jnp.clip(ssum[dst], MIN_NORM)
        xj = jnp.take(logx, src, axis=1).transpose(1, 0, 2)
        out = jax.ops.segment_sum(xj * a[:, :, None], dst, num_segments=n)
        out = out.transpose(1, 0, 2).reshape(n, H * DH) + b_conv
        out = jax.nn.relu(out)
        return proj(expmap0(out))

    def _L3_gnn_ref(x, edge_index, edge_type, weight, bias):
        import jax, jax.numpy as jnp
        import numpy as np
        N_NODES = 3125
        N_EDGES = 50000
        D_IN = 256
        D_OUT = 256
        N_REL = 8
        num_nodes = x.shape[0]
        row, col = (edge_index[0], edge_index[1])
        xt = jnp.einsum('ni,rio->rno', x, weight)
        messages = xt[edge_type, col]
        out = jax.ops.segment_sum(messages, row, num_segments=num_nodes)
        return jax.nn.relu(out + bias)
    edge_index = jnp.stack([src, dst])
    x = _layernorm(x + _L0_gnn_ref(x, src, dst, edge_weight, edge_weight_n2, L0_gnn_gamma, L0_gnn_beta, L0_gnn_W_in, L0_gnn_b_in, L0_gnn_W_out, L0_gnn_b_out, L0_gnn_W_x2i, L0_gnn_b_x2i, L0_gnn_W_h2h), axis=-1)
    x = _layernorm(x + _L1_gnn_ref(x, L1_gnn_basis, L1_gnn_w_comp, L1_gnn_bias, src, dst, edge_type_8), axis=-1)
    x = _layernorm(x + _L2_gnn_ref(x, edge_index, L2_gnn_W, L2_gnn_b_lin, L2_gnn_att, L2_gnn_b_conv), axis=-1)
    x = _layernorm(x + _L3_gnn_ref(x, edge_index, edge_type_8, L3_gnn_weight, L3_gnn_bias), axis=-1)
    return x

_drawn_inputs = setup_inputs


def setup_inputs(seed=0):
    import zlib

    import numpy as np

    out = dict(_drawn_inputs(seed))
    spreads = {'L0_gnn_gamma': (1.0, 0.2),
     'L0_gnn_beta': (0.0, 0.1),
     'L2_gnn_b_conv': (0.0, 0.1),
     'L3_gnn_bias': (0.0, 0.435)}
    factors = {'L1_gnn_bias': 55.709, 'L2_gnn_b_lin': 64.0, 'L2_gnn_att': 8.0}
    for name, (base, spread) in spreads.items():
        noise = np.random.default_rng([zlib.crc32(name.encode()), seed]).standard_normal(out[name].shape)
        drawn = base * np.exp(spread * noise) if base else spread * noise
        out[name] = jnp.asarray(drawn.astype(out[name].dtype))
    for name, factor in factors.items():
        out[name] = (out[name] * factor).astype(out[name].dtype)
    return out
```

```python
from contextlib import ExitStack

import numpy as np
import concourse.bass as bass
from concourse import mybir

F32 = mybir.dt.float32
BF16 = mybir.dt.bfloat16
I32 = mybir.dt.int32
I16 = mybir.dt.int16
ALU = mybir.AluOpType
ACT = mybir.ActivationFunctionType
AX = mybir.AxisListType

P = 128
N = 3125
E = 100000
D = 256
R = 8
NB = 4
H = 4
DH = D // H
T = -(-N // P)
NP = T * P
LAST = N - (T - 1) * P
BUCKETS = T + 1
GRP = 4
RING = 4
BODY = GRP * RING
EC = -(-E // (P * BODY)) * BODY
EH = EC // 2
PAIRS = -(-E // (2 * P)) + T
CH = -(-2 * PAIRS // BODY) * BODY
CHP = -(-(P * EC + BUCKETS * (2 * P - 1)) // (2 * P)) * 2 + GRP
LOOPS = CH // BODY
EPS = 1e-5
MAXN = 1.0 - 0.004
LARGEST = float(np.float32(1.0 - 1e-7))
FAR = -1e30


class Count:

    def __init__(self, eng, sem):
        self.eng, self.sem, self.n, self.base, self.k = eng, sem, 0, None, 0

    def step(self, ins):
        ins.then_inc(self.sem, 1)
        if self.base is None:
            self.n += 1
        else:
            self.k += 1

    def value(self):
        return self.n if self.base is None else self.base + self.k

    def wait(self):
        self.eng.wait_ge(self.sem, self.value())

    def enter(self, i, per):
        self.base, self.k, self.per = i * per + self.n, 0, per

    def leave(self, count):
        assert self.k == self.per, (self.k, self.per)
        self.n, self.base = self.n + count * self.per, None


class Mem:

    def __init__(self, nc, ctx, tag):
        self.nc, self.ctx, self.tag, self.sems = nc, ctx, tag, []
        ctx.callback(self.clear)

    def clear(self):
        if self.sems:
            self.nc.clear_and_free_semaphores(self.sems)
            self.nc.all_engine_barrier()

    def sb(self, name, shape, dt=F32):
        return self.ctx.enter_context(self.nc.sbuf_tensor(f"{self.tag}_{name}", shape, dt))

    def ps(self, name, shape, dt=F32):
        return self.ctx.enter_context(self.nc.psum_tensor(f"{self.tag}_{name}", shape, dt))

    def sem(self, name):
        self.sems.append(self.nc.alloc_semaphore(f"{self.tag}_{name}"))
        return self.sems[-1]


class Shared:
    pass


def make_constants(nc, g):
    with ExitStack() as ctx:
        m = Mem(nc, ctx, "const")
        made = m.sem("made")
        nums = m.sb("nums", [P, CHP], I32)
        pair_nums = m.sb("pair_nums", [P, CHP // 2], I32)
        block = ctx.enter_context(nc.Block())

        @block.gpsimd
        def _(pool):
            nc.gpsimd.iota(nums[:], [[1, CHP]], base=0, channel_multiplier=0).then_inc(made, 1)
            nc.gpsimd.iota(pair_nums[:], [[2 * P, CHP // 2]], base=0, channel_multiplier=0).then_inc(made, 1)
            nc.gpsimd.memset(g.ident[:], 0.0).then_inc(made, 1)
            nc.gpsimd.memset(g.minus_upto[:], -1.0).then_inc(made, 1)
            nc.gpsimd.memset(g.ones_b[:], 1.0)
            nc.gpsimd.memset(g.ones_f[:], 1.0)
            pool.wait_ge(made, 4)
            nc.gpsimd.tensor_copy(g.iota[:], nums[:])
            nc.gpsimd.tensor_copy(g.pair_start[:], pair_nums[:])
            nc.gpsimd.affine_select(out=g.ident[:], in_=g.ident[:], compare_op=ALU.not_equal, fill=1.0,
                                    base=0, pattern=[[-1, P]], channel_multiplier=1)
            nc.gpsimd.affine_select(out=g.minus_upto[:], in_=g.minus_upto[:], compare_op=ALU.is_ge, fill=0.0,
                                    base=0, pattern=[[-1, P]], channel_multiplier=1)


def sort_edges(nc, g, src, dst, etype, w_in, w_out):
    rec_dram = [nc.dram_tensor(f"records_by_{k}", (P * CHP, 4), F32) for k in ("dst", "src")]
    with ExitStack() as ctx:
        m = Mem(nc, ctx, "sort")
        e_end = [m.sb("e_dst", [P, EC], I32), m.sb("e_src", [P, EC], I32)]
        e_type = m.sb("e_type", [P, EC], I32)
        e_w = [m.sb("e_w_in", [P, EC]), m.sb("e_w_out", [P, EC])]
        empty = m.sb("empty", [P, CHP, 4])
        records = [m.sb(f"records_{k}", [P, EC, 4]) for k in range(2)]
        place = [m.sb(f"place_{k}", [P, EC], I32) for k in range(2)]
        tile_no = m.sb("tile_no", [P, EC], I32)
        local = m.sb("local", [P, EC], I32)
        hot = m.sb("hot", [P, EC], BF16)
        zeros = m.sb("zeros", [P, EH])
        running = m.sb("running", [P, EC])
        rank = m.sb("rank", [P, EC])
        pos = m.sb("pos", [P, EC])
        pos_i = m.sb("pos_i", [P, EC], I32)
        base = m.sb("base", [P, 1])
        end_i = m.sb("end_i", [P, 2], I32)
        tile_count = m.sb("tile_count", [P, CHP // 2])
        ring_rec = m.sb("ring_rec", [P, BODY, 4])
        ring_place = m.sb("ring_place", [P, BODY], I32)
        before = m.ps("before", [P, 2, 512])
        total = m.ps("total", [P, 2, 512])

        filled = m.sem("filled")
        edges_in = m.sem("edges_in")
        emptied = m.sem("emptied")
        hot_ready = m.sem("hot_ready")
        ranked = m.sem("ranked")
        vec_step = m.sem("vec_step")
        placed = m.sem("placed")
        staged = m.sem("staged")
        tick = m.sem("tick")
        landed = [m.sem(f"landed_{r}") for r in range(RING)]
        rec_in = m.sem("rec_in")
        block = ctx.enter_context(nc.Block())

        full = P - 1
        rest = E - full * EC
        steps = EC // BODY

        @block.sync
        def _(sp):
            sp.wait_ge(filled, 1)
            for tile, arr in ((e_end[0], dst), (e_end[1], src), (e_type, etype), (e_w[0], w_in), (e_w[1], w_out)):
                sp.dma_start(tile[0:full, :], arr[0:full * EC].rearrange("(p c) -> p c", c=EC)).then_inc(edges_in, 16)
                sp.dma_start(tile[full:P, 0:rest], arr[full * EC:E].rearrange("(p c) -> p c", p=1)).then_inc(edges_in, 16)
            sp.wait_ge(filled, 2)
            for k in range(2):
                sp.dma_start(rec_dram[k].ap().rearrange("(p c) w -> p (c w)", p=P),
                             empty[:].rearrange("p c w -> p (c w)")).then_inc(emptied, 16)
            for k in range(2):
                for r in range(RING):
                    sp.wait_ge(landed[r], 16 * GRP * steps * (k + 1))
                sp.dma_start(g.rec[k][:].rearrange("p c w -> p (c w)"),
                             rec_dram[k].ap().rearrange("(p c) w -> p (c w)", p=P)).then_inc(rec_in, 16)
            sp.wait_ge(rec_in, 32)

        @block.vector
        def _(dve):
            nc.vector.memset(e_end[0][:], NP)
            nc.vector.memset(e_end[1][:], NP)
            nc.vector.memset(e_type[:], 0)
            nc.vector.memset(e_w[0][:], 0.0)
            nc.vector.memset(e_w[1][:], 0.0).then_inc(filled, 1)
            c = Count(dve, vec_step)
            c.step(nc.vector.memset(empty[:], 0.0))
            c.wait()
            nc.vector.memset(empty[:, :, 2], -1.0).then_inc(filled, 1)
            nc.vector.memset(zeros[:], 0.0)
            dve.wait_ge(edges_in, 160)
            for k in range(2):
                key, other, rec = e_end[k], e_end[1 - k], records[k]
                nc.vector.memset(tile_count[:], 0.0)
                nc.vector.memset(base[:], 0.0)
                nc.vector.memset(pos[:], 0.0)
                nc.vector.tensor_scalar(tile_no[:], key[:], 7, None, ALU.arith_shift_right)
                nc.vector.tensor_scalar(local[:], key[:], P - 1, None, ALU.bitwise_and)
                nc.vector.tensor_scalar(rec[:, :, 0], other[:], float(N - 1), None, ALU.min)
                nc.vector.tensor_copy(rec[:, :, 3], e_w[k][:])
                c.step(nc.vector.scalar_tensor_tensor(rank[:], other[:], float(R), e_type[:], ALU.mult, ALU.add))
                c.wait()
                nc.vector.tensor_copy(rec[:, :, 2], local[:])
                c.step(nc.vector.tensor_scalar(rec[:, :, 1], rank[:], float(N * R - 1), None, ALU.min))
                c.wait()
                with dve.Fori(0, BUCKETS) as b:
                    c.enter(b, 8)
                    nc.vector.tensor_scalar(hot[:], tile_no[:], g.iota[:, bass.ds(b, 1)], None,
                                            ALU.is_equal).then_inc(hot_ready, 1)
                    dve.wait_ge(ranked, b + (1 + BUCKETS * k))
                    for h in range(2):
                        c.step(nc.vector.tensor_tensor_scan(
                            running[:, h * EH:(h + 1) * EH], total[:, h, 0:EH], zeros[:],
                            base[:] if h == 0 else running[:, EH - 1:EH], ALU.add, ALU.max))
                        c.wait()
                    c.step(nc.vector.tensor_tensor(rank[:].rearrange("p (h c) -> p h c", h=2),
                                                   running[:].rearrange("p (h c) -> p h c", h=2),
                                                   before[:, :, 0:EH], ALU.add))
                    c.step(nc.vector.tensor_scalar(end_i[:, 0:1], running[:, EC - 1:EC], float(2 * P - 1), None,
                                                   ALU.add))
                    c.wait()
                    c.step(nc.vector.tensor_scalar(end_i[:, 1:2], end_i[:, 0:1], 8, 8, ALU.arith_shift_right,
                                                   ALU.arith_shift_left))
                    c.wait()
                    nc.vector.tensor_copy(base[:], end_i[:, 1:2])
                    c.step(nc.vector.copy_predicated(pos[:], hot[:].bitcast(I16), rank[:]))
                    c.wait()
                    c.step(nc.vector.scalar_tensor_tensor(tile_count[:], g.pair_start[:], base[:], tile_count[:],
                                                          ALU.is_ge, ALU.add))
                    c.wait()
                    c.step(nc.vector.tensor_copy(end_i[:, 0:1], end_i[:, 1:2]))
                c.leave(BUCKETS)
                nc.vector.tensor_scalar(g.pair_tile[k][:], tile_count[:], float(T), None, ALU.min)
                c.step(nc.vector.tensor_copy(pos_i[:], pos[:]))
                c.wait()
                nc.vector.tensor_scalar(tile_no[:], pos_i[:], 7, None, ALU.arith_shift_right)
                c.step(nc.vector.tensor_scalar(local[:], pos_i[:], P - 1, None, ALU.bitwise_and))
                c.wait()
                c.step(nc.vector.scalar_tensor_tensor(place[k][:], local[:], float(CHP), tile_no[:], ALU.mult,
                                                      ALU.add))
                c.wait()
                dve.sem_inc(placed, 1)

        @block.tensor
        def _(pe):
            for k in range(2):
                with pe.Fori(0, BUCKETS) as b:
                    pe.wait_ge(hot_ready, b + (1 + BUCKETS * k))
                    for h in range(2):
                        nc.tensor.matmul(before[:, h, 0:EH], g.minus_upto[:], hot[:, h * EH:(h + 1) * EH],
                                         start=True, stop=True)
                    for h in range(2):
                        last = nc.tensor.matmul(total[:, h, 0:EH], g.ones_b[:], hot[:, h * EH:(h + 1) * EH],
                                                start=True, stop=True)
                    last.then_inc(ranked, 1)

        @block.scalar
        def _(act):
            def stage(k, at, r):
                s = slice(r * GRP, (r + 1) * GRP)
                nc.scalar.copy(ring_place[:, s], place[k][:, bass.ds(at, GRP)])
                nc.scalar.copy(ring_rec[:, s, :], records[k][:, bass.ds(at, GRP), :]).then_inc(staged, 1)

            for k in range(2):
                act.wait_ge(placed, k + 1)
                for r in range(RING):
                    if k:
                        act.wait_ge(landed[r], 16 * GRP * steps)
                    stage(k, r * GRP, r)
                with act.Fori(1, steps) as i:
                    for r in range(RING):
                        act.wait_ge(landed[r], i * (16 * GRP) + 16 * GRP * steps * k)
                        stage(k, i * BODY + r * GRP, r)

        @block.gpsimd
        def _(pool):
            pool.wait_ge(emptied, 32)
            for k in range(2):
                with pool.Fori(0, steps) as i:
                    for r in range(RING):
                        pool.wait_ge(staged, i * RING + (r + 1 + RING * steps * k))
                        pool.sem_inc(tick, 1)
                        for j in range(r * GRP, (r + 1) * GRP):
                            pool.indirect_dma_start(rec_dram[k].ap(), bass.IndirectOffsetOnAxis(
                                ap=ring_place[:, j:j + 1], axis=0), ring_rec[:, j, :], None).then_inc(landed[r], 16)


def aggregate(nc, g, tag, k, table, words, word, acc, weighted, ones_column):
    width = words + ones_column
    with ExitStack() as ctx:
        m = Mem(nc, ctx, tag)
        rows = m.sb("rows", [P, BODY, width])
        hot = m.sb("hot", [P, BODY, P])
        ring_row = m.sb("ring_row", [P, BODY], I32)
        sums = m.ps("sums", [P, 2 * RING, 512])
        ready = m.sem("ready")
        staged = m.sem("staged")
        tick = m.sem("tick")
        hot_ready = m.sem("hot_ready")
        summed = m.sem("summed")
        psum_free = m.sem("psum_free")
        added = m.sem("added")
        landed = [m.sem(f"landed_{r}") for r in range(RING)]
        block = ctx.enter_context(nc.Block())

        @block.scalar
        def _(act):
            def stage(at, r):
                nc.scalar.copy(ring_row[:, r * GRP:(r + 1) * GRP],
                               g.rec[k][:, bass.ds(at, GRP), word]).then_inc(staged, 1)

            for r in range(RING):
                stage(r * GRP, r)
            with act.Fori(1, LOOPS) as i:
                for r in range(RING):
                    act.wait_ge(summed, i * RING + (r + 1 - RING))
                    stage(i * BODY + r * GRP, r)

        @block.gpsimd
        def _(pool):
            if ones_column:
                nc.gpsimd.memset(rows[:, :, words:width], 1.0).then_inc(ready, 1)
            with pool.Fori(0, LOOPS) as i:
                for r in range(RING):
                    pool.wait_ge(staged, i * RING + (r + 1))
                    pool.sem_inc(tick, 1)
                    for j in range(r * GRP, (r + 1) * GRP):
                        pool.indirect_dma_start(rows[:, j, 0:words], None, table, bass.IndirectOffsetOnAxis(
                            ap=ring_row[:, j:j + 1], axis=0)).then_inc(landed[r], 16)

        @block.tensor
        def _(pe):
            if ones_column:
                pe.wait_ge(ready, 1)
            with pe.Fori(0, LOOPS) as i:
                for r in range(RING):
                    pe.wait_ge(landed[r], i * (16 * GRP) + 16 * GRP)
                    pe.wait_ge(hot_ready, i * RING + (r + 1))
                    pe.wait_ge(psum_free, i * RING + (r + 1))
                    for q in range(GRP):
                        j = r * GRP + q
                        last = nc.tensor.matmul(sums[:, 2 * r + q // 2, 0:width], hot[:, j, :], rows[:, j, :],
                                                start=q % 2 == 0, stop=q % 2 == 1)
                    last.then_inc(summed, 1)

        @block.vector
        def _(dve):
            def build(at, r):
                for q in range(GRP):
                    last = nc.vector.tensor_scalar(
                        hot[:, r * GRP + q, :], g.iota[:, 0:P], g.rec[k][:, bass.ds(at + q, 1), 2],
                        g.rec[k][:, bass.ds(at + q, 1), 3] if weighted else None,
                        ALU.is_equal, ALU.mult if weighted else ALU.bypass)
                last.then_inc(hot_ready, 1)

            dve.sem_inc(psum_free, RING)
            build(0, 0)
            with dve.Fori(0, LOOPS) as i:
                for r in range(RING):
                    build(i * BODY + (r + 1) * GRP, (r + 1) % RING)
                    tiles = [dve.value_load(g.pair_tile[k][0:1, bass.ds(i * (BODY // 2) + (2 * r + q), 1)],
                                            min_val=0, max_val=T) for q in range(2)]
                    dve.wait_ge(summed, i * RING + (r + 1))
                    for q in range(2):
                        if r + q:
                            dve.wait_ge(added, i * (2 * RING) + (2 * r + q))
                        at = acc[:, bass.ds(tiles[q], 1), 0:width].rearrange("p t d -> p (t d)")
                        last = nc.vector.tensor_tensor(at, sums[:, 2 * r + q, 0:width], at, ALU.add)
                        last.then_inc(added, 1)
                    dve.wait_ge(added, i * (2 * RING) + (2 * r + 2))
                    dve.sem_inc(psum_free, 1)


class Vector:

    def __init__(self, nc, dve, count, roots=None):
        self.nc, self.dve, self.c, self.roots, self.asked = nc, dve, count, roots, 0

    def did(self, ins):
        self.c.step(ins)
        self.c.wait()

    def ts(self, out, x, s0, op0, s1=None, op1=ALU.bypass):
        self.did(self.nc.vector.tensor_scalar(out, x, s0, s1, op0, op1))

    def tt(self, out, x, y, op):
        self.did(self.nc.vector.tensor_tensor(out, x, y, op))

    def stt(self, out, x, s, y, op0, op1):
        self.did(self.nc.vector.scalar_tensor_tensor(out, x, s, y, op0, op1))

    def recip(self, out, x):
        self.did(self.nc.vector.reciprocal(out, x))

    def row_sum(self, out, x):
        self.did(self.nc.vector.tensor_reduce(out, x, AX.X, ALU.add))

    def sqrt(self, out, x, tmp):
        self.asked += 1
        self.dve.sem_inc(self.roots.asked, 1)
        self.dve.wait_ge(self.roots.given, self.asked)
        self.ts(out, out, 1e-30, ALU.max)
        self.recip(tmp, out)
        self.tt(tmp, tmp, x, ALU.mult)
        self.tt(out, out, tmp, ALU.add)
        self.ts(out, out, 0.5, ALU.mult)

    def to_one(self, scale, norm, most, tmp):
        self.recip(tmp, norm)
        self.ts(tmp, tmp, most, ALU.mult, 1.0, ALU.min)
        self.tt(scale, scale, tmp, ALU.mult)


class Roots:

    def __init__(self, nc, m):
        self.nc, self.asked, self.given, self.k = nc, m.sem("root_asked"), m.sem("root_given"), 0

    def root(self, act, out, x):
        self.k += 1
        act.wait_ge(self.asked, self.k)
        self.nc.scalar.activation(out, x, ACT.Sqrt).then_inc(self.given, 1)


class NormTiles:
    def __init__(self, m):
        self.stats = m.sb("stats", [P, T, 6])
        self.mean, self.var, self.tmp, self.root = (m.sb(n, [P, T]) for n in ("ln_mean", "ln_var", "ln_tmp", "ln_root"))


def row_of_all(ap):
    return ap.partition_broadcast(P)


def over_tiles(ap):
    return ap.unsqueeze(1).broadcast_to([P, T, ap.shape[1]])


def over_features(ap, n=D):
    return ap.unsqueeze(2).broadcast_to([*ap.shape, n])


def normalise(nc, g, ln, dve, c, v):
    stats, mean, var, tmp = ln.stats, ln.mean, ln.var, ln.tmp
    with dve.Fori(0, T) as t:
        c.enter(t, 1)
        c.step(nc.vector.bn_stats(stats[:, bass.ds(t, 1), :].rearrange("p t s -> p (t s)"),
                                  g.x[:, bass.ds(t, 1), :].rearrange("p t d -> p (t d)")))
    c.leave(T)
    c.wait()
    v.tt(mean[:], stats[:, :, 1], stats[:, :, 4], ALU.add)
    v.tt(tmp[:], stats[:, :, 1], stats[:, :, 4], ALU.subtract)
    v.tt(var[:], stats[:, :, 2], stats[:, :, 5], ALU.add)
    v.tt(tmp[:], tmp[:], tmp[:], ALU.mult)
    v.stt(var[:], tmp[:], float(D) / 4, var[:], ALU.mult, ALU.add)
    v.ts(mean[:], mean[:], 0.5, ALU.mult)
    v.ts(var[:], var[:], 1.0 / D, ALU.mult, EPS, ALU.add)
    v.sqrt(ln.root[:], var[:], tmp[:])
    v.recip(var[:], ln.root[:])
    v.tt(g.x[:], g.x[:], over_features(mean[:]), ALU.subtract)
    v.tt(g.x[:], g.x[:], over_features(var[:]), ALU.mult)


def load_and_batch_norm(nc, g, a, h_dram):
    with ExitStack() as ctx:
        m = Mem(nc, ctx, "bn")
        gamma, beta, mean, rstd = (m.sb(n, [P, D]) for n in ("gamma", "beta", "mean", "rstd"))
        ones_last = m.sb("ones_last", [P, P])
        sums = m.ps("sums", [P, 2, 512])
        cleared, loaded, masked, summed, centred, squared, vec, ready, stored = (m.sem(n) for n in (
            "cleared", "loaded", "masked", "summed", "centred", "squared", "vec", "ready", "stored"))
        square = g.acc[:, 0:T, 0:D]
        var, tmp = m.sb("var", [P, D]), m.sb("tmp", [P, D])
        roots = Roots(nc, m)
        block = ctx.enter_context(nc.Block())

        @block.sync
        def _(sp):
            sp.wait_ge(cleared, 1)
            sp.dma_start(g.x[:, 0:T - 1, :],
                         a["x"][0:(T - 1) * P, :].rearrange("(t p) d -> p t d", p=P)).then_inc(loaded, 16)
            sp.dma_start(g.x[0:LAST, T - 1, :], a["x"][(T - 1) * P:N, :]).then_inc(loaded, 16)
            sp.dma_start(gamma[:], row_of_all(a["L0_gnn_gamma"])).then_inc(loaded, 16)
            sp.dma_start(beta[:], row_of_all(a["L0_gnn_beta"])).then_inc(loaded, 16)
            sp.wait_ge(ready, 1)
            sp.dma_start(h_dram.ap().rearrange("(t p) d -> p t d", p=P), g.h).then_inc(stored, 16)
            sp.wait_ge(stored, 16)

        @block.gpsimd
        def _(pool):
            nc.gpsimd.memset(ones_last[:], 1.0).then_inc(masked, 1)
            pool.wait_ge(masked, 1)
            nc.gpsimd.affine_select(out=ones_last[:], in_=ones_last[:], compare_op=ALU.is_gt, fill=0.0,
                                    base=LAST, pattern=[[0, P]], channel_multiplier=-1).then_inc(masked, 1)

        @block.tensor
        def _(pe):
            pe.wait_ge(loaded, 64)
            for t in range(T):
                last = nc.tensor.matmul(sums[:, 0, 0:D], g.ones_f[:], g.x[:, t, :], start=t == 0, stop=t == T - 1)
            last.then_inc(summed, 1)
            pe.wait_ge(masked, 2)
            pe.wait_ge(squared, 1)
            for t in range(T):
                last = nc.tensor.matmul(sums[:, 1, 0:D], ones_last[:] if t == T - 1 else g.ones_f[:],
                                        square[:, t, :], start=t == 0, stop=t == T - 1)
            last.then_inc(summed, 1)

        @block.scalar
        def _(act):
            act.wait_ge(centred, 1)
            nc.scalar.activation(square, g.h, ACT.Square).then_inc(squared, 1)
            roots.root(act, rstd[:], var[:])

        @block.vector
        def _(dve):
            c = Count(dve, vec)
            v = Vector(nc, dve, c, roots)
            nc.vector.memset(g.x[:, T - 1, :], 0.0).then_inc(cleared, 1)
            dve.wait_ge(summed, 1)
            v.ts(mean[:], sums[:, 0, 0:D], 1.0 / N, ALU.mult)
            nc.vector.tensor_tensor(g.h, g.x[:], over_tiles(mean[:]), ALU.subtract).then_inc(centred, 1)
            dve.wait_ge(summed, 2)
            v.ts(var[:], sums[:, 1, 0:D], 1.0 / N, ALU.mult, EPS, ALU.add)
            v.sqrt(rstd[:], var[:], tmp[:])
            v.recip(rstd[:], rstd[:])
            v.tt(rstd[:], rstd[:], gamma[:], ALU.mult)
            v.tt(g.h, g.h, over_tiles(rstd[:]), ALU.mult)
            nc.vector.tensor_tensor(g.h, g.h, over_tiles(beta[:]), ALU.add).then_inc(ready, 1)
            nc.vector.memset(g.acc[:], 0.0)
            nc.vector.memset(g.acc2, 0.0)


def gated_update(nc, g, a):
    with ExitStack() as ctx:
        m = Mem(nc, ctx, "gate")
        w_first = m.sb("w_first", [P, 2, 2, D])
        w_x = m.sb("w_x", [P, 4, 2 * D])
        w_all = m.sb("w_all", [P, 6, 2 * D])
        b_cols = m.sb("b_cols", [P, 4, 3])
        unit = m.sb("unit", [1, 3])
        b_x = m.sb("b_x", [1, 2 * D])
        b_all = m.sb("b_all", [3, 2 * D])
        tile = m.sb("tile", [P, 3, D])
        sides = m.sb("sides", [P, T, 3])
        side = m.sb("side", [P, 3])
        turned = m.sb("turned", [P, 6, P])
        side_t = m.sb("side_t", [3, P])
        gate = m.sb("gate", [P, 2, D])
        tmp = m.sb("tmp", [P, D])
        roots, ln = Roots(nc, m), NormTiles(m)
        p_w = m.ps("p_w", [P, 512])
        p_t = m.ps("p_t", [P, 6, P])
        p_s = m.ps("p_s", [P, 512])
        p_g = m.ps("p_g", [P, 512])
        cleared, loaded, product, copied, staged, turn, back, gates, acted, vec, done = (m.sem(n) for n in (
            "cleared", "loaded", "product", "copied", "staged", "turn", "back", "gates", "acted", "vec", "done"))
        block = ctx.enter_context(nc.Block())

        @block.sync
        def _(sp):
            sp.wait_ge(cleared, 1)
            for n, w in enumerate(("L0_gnn_W_in_T", "L0_gnn_W_out_T")):
                sp.dma_start(w_first[:, n, :, :], a[w].rearrange("(s p) i -> p s i", p=P)).then_inc(loaded, 16)
            sp.dma_start(w_x[:], a["L0_gnn_W_x2i"].rearrange("(s p) i -> p s i", p=P)).then_inc(loaded, 16)
            sp.dma_start(w_all[:, 4:6, :], a["L0_gnn_W_h2h"].rearrange("(s p) i -> p s i", p=P)).then_inc(loaded, 16)
            for n, b in enumerate(("L0_gnn_b_in", "L0_gnn_b_out")):
                for s in range(2):
                    sp.dma_start(b_cols[:, 2 * n + s, n:n + 1],
                                 a[b][s * P:(s + 1) * P].rearrange("(p a) -> p a", a=1)).then_inc(loaded, 16)
            sp.dma_start(b_x[:], a["L0_gnn_b_x2i"].rearrange("(a d) -> a d", a=1)).then_inc(loaded, 16)

        @block.tensor
        def _(pe):
            pe.wait_ge(loaded, 144)
            for n in range(2):
                for i in range(2):
                    if n + i:
                        pe.wait_ge(copied, 2 * n + i)
                    for s in range(2):
                        last = nc.tensor.matmul(p_w[:], w_first[:, n, s, i * P:(i + 1) * P], w_x[:, 2 * n + s, :],
                                                start=s == 0, stop=s == 1)
                    last.then_inc(product, 1)
            for s in range(4):
                nc.tensor.matmul(p_g[0:3, :], b_cols[:, s, :], w_x[:, s, :], start=s == 0, stop=False)
            nc.tensor.matmul(p_g[0:3, :], unit[:], b_x[:], start=False, stop=True).then_inc(product, 1)
            pe.wait_ge(copied, 5)
            with pe.Fori(0, T) as t:
                pe.wait_ge(staged, t * 3 + 3)
                for s in range(6):
                    nc.tensor.transpose(p_t[:, s, :], tile[:, s // 2, (s % 2) * P:(s % 2 + 1) * P], g.ident[:])
                nc.tensor.transpose(p_s[0:3, 0:P], side[:], g.ident[:]).then_inc(turn, 1)
                pe.wait_ge(back, t * 2 + 2)
                pe.wait_ge(acted, t + 1)
                for s in range(6):
                    nc.tensor.matmul(p_g[:], turned[:, s, :], w_all[:, s, :], start=s == 0, stop=False)
                nc.tensor.matmul(p_g[:], side_t[:], b_all[:], start=False, stop=True).then_inc(gates, 1)

        @block.scalar
        def _(act):
            act.sem_inc(acted, 1)
            with act.Fori(0, T) as t:
                act.wait_ge(turn, t + 1)
                nc.scalar.copy(tile[:, 0, :], g.acc[:, bass.ds(t, 1), 0:D].rearrange("p t d -> p (t d)")).then_inc(staged, 1)
                nc.scalar.copy(tile[:, 1, :], g.acc2[:, bass.ds(t, 1), 0:D].rearrange("p t d -> p (t d)")).then_inc(staged, 1)
                act.wait_ge(turn, t + 2)
                nc.scalar.copy(turned[:, 0:4, :], p_t[:, 0:4, :]).then_inc(back, 1)
                act.wait_ge(gates, t + 1)
                act.wait_ge(done, t + 1)
                nc.scalar.activation(gate[:, 0, :], p_g[:, 0:D], ACT.Tanh, scale=0.5)
                nc.scalar.activation(gate[:, 1, :], p_g[:, D:2 * D], ACT.Tanh).then_inc(acted, 1)
            roots.root(act, ln.root[:], ln.var[:])

        @block.vector
        def _(dve):
            c = Count(dve, vec)
            v = Vector(nc, dve, c, roots)
            nc.vector.memset(b_cols[:], 0.0)
            nc.vector.memset(unit[:], 0.0)
            v.did(nc.vector.memset(sides[:, :, 2], 1.0))
            nc.vector.memset(unit[:, 2:3], 1.0).then_inc(cleared, 1)
            nc.vector.tensor_copy(sides[:, :, 0], g.acc[:, 0:T, D])
            v.did(nc.vector.tensor_copy(sides[:, :, 1], g.acc2[:, 0:T, D]))
            dve.sem_inc(turn, 1)
            dve.sem_inc(done, 1)
            for s in range(4):
                dve.wait_ge(product, s + 1)
                nc.vector.tensor_copy(w_all[:, s, :], p_w[:]).then_inc(copied, 1)
            dve.wait_ge(product, 5)
            nc.vector.tensor_copy(b_all[:], p_g[0:3, :]).then_inc(copied, 1)
            with dve.Fori(0, T) as t:
                c.enter(t, 7)
                x = g.x[:, bass.ds(t, 1), :].rearrange("p t d -> p (t d)")
                dve.wait_ge(turn, t + 1)
                c.step(nc.vector.tensor_copy(side[:], sides[:, bass.ds(t, 1), :].rearrange("p t d -> p (t d)")))
                c.wait()
                nc.vector.tensor_copy(tile[:, 2, :], g.h[:, bass.ds(t, 1), :].rearrange("p t d -> p (t d)")).then_inc(staged, 1)
                dve.wait_ge(turn, t + 2)
                v.did(nc.vector.tensor_copy(side_t[:], p_s[0:3, 0:P]))
                nc.vector.tensor_copy(turned[:, 4:6, :], p_t[:, 4:6, :]).then_inc(back, 1)
                dve.wait_ge(acted, t + 2)
                v.ts(gate[:, 0, :], gate[:, 0, :], 0.5, ALU.mult, 0.5, ALU.add)
                v.tt(tmp[:], tile[:, 2, :], gate[:, 1, :], ALU.subtract)
                v.tt(tmp[:], tmp[:], gate[:, 0, :], ALU.mult)
                v.tt(tmp[:], tmp[:], gate[:, 1, :], ALU.add)
                v.tt(x, x, tmp[:], ALU.add)
                dve.sem_inc(done, 1)
            c.leave(T)
            normalise(nc, g, ln, dve, c, v)


def relation_tables(nc, g, a, tag, t_dram, relational):
    parts = 2 if relational else 1
    with ExitStack() as ctx:
        m = Mem(nc, ctx, tag)
        w = m.sb("w", [P, parts, R, D])
        mix = m.sb("mix", [P, 2, P])
        comp = m.sb("comp", [P, NB])
        tile = m.sb("tile", [P, D])
        turned = m.sb("turned", [P, 2, P])
        mixed = m.sb("mixed", [P, P])
        table = m.sb("table", [P, 2, R, D])
        p_t = m.ps("p_t", [P, 2, P])
        p_m = m.ps("p_m", [P, P])
        p_o = m.ps("p_o", [P, 4, 2, D])
        loaded, made, staged, turn, back, mixing, unmixed, product, low_out, high_out = (m.sem(n) for n in (
            "loaded", "made", "staged", "turn", "back", "mixing", "unmixed", "product", "low_out", "high_out"))
        stored = [m.sem(f"stored_{q}") for q in range(2)]
        loads = 16 * (2 if relational else 1 + P // R)
        block = ctx.enter_context(nc.Block())

        @block.sync
        def _(sp):
            if relational:
                for s in range(2):
                    sp.dma_start(w[:, s, :, :], a["L3_gnn_weight"][:, s * P:(s + 1) * P, :]
                                 .rearrange("r p o -> p r o")).then_inc(loaded, 16)
            else:
                sp.dma_start(w[:, 0, :, :], a["L1_gnn_basis"].rearrange("b i o -> (b i) o")
                             .rearrange("(r p) o -> p r o", p=P)).then_inc(loaded, 16)
                for n in range(P // R):
                    sp.dma_start(comp[n * R:(n + 1) * R, :], a["L1_gnn_w_comp"]).then_inc(loaded, 16)
            def store(t, q):
                sp.wait_ge(low_out, t + 2)
                sp.wait_ge(high_out, t + 2)
                sp.dma_start(t_dram.ap()[bass.ds(t * (P * R), P * R), :].rearrange("(p r) d -> p (r d)", r=R),
                             table[:, q, :, :].rearrange("p r d -> p (r d)")).then_inc(stored[q], 16)

            with sp.Fori(0, T // 2) as t:
                for q in range(2):
                    store(t * 2 + q, q)
            store(T - 1, 0)
            sp.wait_ge(stored[0], 16 * (T // 2 + 1))
            sp.wait_ge(stored[1], 16 * (T // 2))

        @block.gpsimd
        def _(pool):
            if not relational:
                pool.wait_ge(loaded, loads)
                for s in range(2):
                    nc.gpsimd.tensor_copy(mix[:, s, :].rearrange("p (j b) -> p j b", b=NB),
                                          comp[:].unsqueeze(1).broadcast_to([P, P // NB, NB])).then_inc(made, 1)
                pool.wait_ge(made, 2)
                for s in range(2):
                    v = mix[:, s, :].rearrange("p (j b) -> p j b", b=NB)
                    nc.gpsimd.affine_select(out=v, in_=v, compare_op=ALU.is_ge, fill=0.0, base=P * s,
                                            pattern=[[-R, P // NB], [0, NB]], channel_multiplier=1).then_inc(made, 1)
                pool.wait_ge(made, 4)
                for s in range(2):
                    v = mix[:, s, :].rearrange("p (j b) -> p j b", b=NB)
                    nc.gpsimd.affine_select(out=v, in_=v, compare_op=ALU.is_ge, fill=0.0, base=R - 1 - P * s,
                                            pattern=[[R, P // NB], [0, NB]], channel_multiplier=-1).then_inc(made, 1)

        @block.tensor
        def _(pe):
            pe.wait_ge(loaded, loads)
            if not relational:
                pe.wait_ge(made, 6)
            with pe.Fori(0, T) as t:
                pe.wait_ge(staged, t + 1)
                for s in range(2):
                    last = nc.tensor.transpose(p_t[:, s, :], tile[:, s * P:(s + 1) * P], g.ident[:])
                last.then_inc(turn, 1)
                pe.wait_ge(back, t + 1)
                if not relational:
                    for s in range(2):
                        last = nc.tensor.matmul(p_m[:], mix[:, s, :], turned[:, s, :], start=s == 0, stop=s == 1)
                    last.then_inc(mixing, 1)
                    pe.wait_ge(unmixed, t + 1)
                pe.wait_ge(low_out, t + 1)
                pe.wait_ge(high_out, t + 1)
                for q in range(4):
                    for s in range(parts):
                        last = nc.tensor.matmul(p_o[:, q, :, :], turned[:, s, :] if relational else mixed[:],
                                                w[:, s, 2 * q:2 * q + 2, :], start=s == 0, stop=s == parts - 1)
                    if q % 2:
                        last.then_inc(product, 1)

        @block.scalar
        def _(act):
            act.sem_inc(low_out, 1)

            def tile_work(t, q, refill):
                act.wait_ge(turn, t + 1)
                nc.scalar.copy(turned[:], p_t[:]).then_inc(back, 1)
                act.wait_ge(product, t * 2 + 1)
                if refill is not None:
                    act.wait_ge(stored[q], refill)
                nc.scalar.copy(table[:, q, 0:4, :], p_o[:, 0:2, :, :].rearrange("p a b d -> p (a b) d")
                               ).then_inc(low_out, 1)

            for q in range(2):
                tile_work(q, q, None)
            with act.Fori(1, T // 2) as i:
                for q in range(2):
                    tile_work(i * 2 + q, q, i * 16)
            tile_work(T - 1, 0, 16 * (T // 2))

        @block.vector
        def _(dve):
            dve.sem_inc(high_out, 1)
            nc.vector.memset(g.acc[:], 0.0)
            nc.vector.tensor_copy(tile[:], g.x[:, 0, :]).then_inc(staged, 1)

            def tile_work(t, q, refill, more):
                if not relational:
                    dve.wait_ge(mixing, t + 1)
                    nc.vector.tensor_copy(mixed[:], p_m[:]).then_inc(unmixed, 1)
                if more:
                    dve.wait_ge(turn, t + 1)
                    nc.vector.tensor_copy(tile[:], g.x[:, bass.ds(t + 1, 1), :].rearrange("p t d -> p (t d)")
                                          ).then_inc(staged, 1)
                dve.wait_ge(product, t * 2 + 2)
                if refill is not None:
                    dve.wait_ge(stored[q], refill)
                nc.vector.tensor_copy(table[:, q, 4:8, :], p_o[:, 2:4, :, :].rearrange("p a b d -> p (a b) d")
                                      ).then_inc(high_out, 1)

            for q in range(2):
                tile_work(q, q, None, True)
            with dve.Fori(1, T // 2) as i:
                for q in range(2):
                    tile_work(i * 2 + q, q, i * 16, True)
            tile_work(T - 1, 0, 16 * (T // 2), False)


def relu_update(nc, g, tag, bias_ap, after=None, out=None):
    with ExitStack() as ctx:
        m = Mem(nc, ctx, tag)
        bias = m.sb("bias", [P, D])
        loaded, vec, ready, stored = m.sem("loaded"), m.sem("vec"), m.sem("ready"), m.sem("stored")
        roots, ln = Roots(nc, m), NormTiles(m)
        block = ctx.enter_context(nc.Block())

        @block.scalar
        def _(act):
            roots.root(act, ln.root[:], ln.var[:])

        @block.sync
        def _(sp):
            sp.dma_start(bias[:], row_of_all(bias_ap)).then_inc(loaded, 16)
            if out is not None:
                sp.wait_ge(ready, 1)
                sp.dma_start(out[0:(T - 1) * P, :].rearrange("(t p) d -> p t d", p=P), g.x[:, 0:T - 1, :]
                             ).then_inc(stored, 16)
                sp.dma_start(out[(T - 1) * P:N, :], g.x[0:LAST, T - 1, :]).then_inc(stored, 16)
                sp.wait_ge(stored, 32)

        @block.vector
        def _(dve):
            c = Count(dve, vec)
            v = Vector(nc, dve, c, roots)
            dve.wait_ge(loaded, 16)
            acc = g.acc[:, 0:T, 0:D]
            v.tt(acc, acc, over_tiles(bias[:]), ALU.add)
            v.ts(acc, acc, 0.0, ALU.max)
            v.tt(g.x[:], g.x[:], acc, ALU.add)
            normalise(nc, g, ln, dve, c, v)
            dve.sem_inc(ready, 1)


def hyperbolic_prepare(nc, g, a, lx_dram, msg_dram, sj_dram):
    with ExitStack() as ctx:
        m = Mem(nc, ctx, "hyp")
        w = m.sb("w", [P, 2, D])
        hb = m.sb("hb", [P, D])
        att = m.sb("att", [P, H, 2 * DH])
        tile = m.sb("tile", [P, D])
        turned = m.sb("turned", [P, 2, P])
        p_t = m.ps("p_t", [P, 4, P])
        p_w = m.ps("p_w", [P, 512])
        loaded, staged, turn, back, product, copied, vec, logs, lx_out, lx_in, scored, tables, thrown, tanhs, lns = (
            m.sem(n) for n in ("loaded", "staged", "turn", "back", "product", "copied", "vec", "logs", "lx_out",
                               "lx_in", "scored", "tables", "thrown", "tanhs", "lns"))
        logs_of = {n: m.sem(f"log_of_{n}") for n in "xur"}
        names = ("xx", "nw", "rr", "ww", "wb", "nx", "fx", "nu", "c", "t1", "t2", "t3", "A", "B", "nr")
        s = {n: m.sb(n, [P, T]) for n in names}
        b = {n: m.sb("b_" + n, [P, 1]) for n in ("bb", "nb", "c", "t1")}
        roots = Roots(nc, m)
        y, tmp = g.y, g.tmp
        block = ctx.enter_context(nc.Block())
        flat = lx_dram.ap().rearrange("n (q d) -> (n q) d", d=DH)

        @block.sync
        def _(sp):
            sp.dma_start(w[:], a["L2_gnn_W_T"].rearrange("(s p) o -> p s o", p=P)).then_inc(loaded, 16)
            sp.dma_start(hb[:], row_of_all(a["L2_gnn_b_lin"])).then_inc(loaded, 16)
            sp.dma_start(att[:].rearrange("p h d -> p (h d)"),
                         row_of_all(a["L2_gnn_att"].rearrange("h d -> (h d)"))).then_inc(loaded, 16)
            sp.wait_ge(logs, 1)
            sp.dma_start(lx_dram.ap().rearrange("(t p) d -> p t d", p=P), y).then_inc(lx_out, 16)
            sp.wait_ge(lx_out, 16)
            for h in range(H):
                sp.dma_start(y[:, 0:T - 1, h * DH:(h + 1) * DH],
                             flat[h * N:h * N + (T - 1) * P, :].rearrange("(t p) d -> p t d", p=P)).then_inc(lx_in, 16)
                sp.dma_start(y[0:LAST, T - 1, h * DH:(h + 1) * DH],
                             flat[h * N + (T - 1) * P:(h + 1) * N, :]).then_inc(lx_in, 16)
            sp.wait_ge(scored, 1)
            sp.wait_ge(lx_in, 128)
            sp.dma_start(msg_dram.ap()[:, 0:D].rearrange("(t p) d -> p t d", p=P), y).then_inc(tables, 16)
            sp.dma_start(msg_dram.ap()[:, D:D + H].rearrange("(t p) d -> p t d", p=P), g.sj[:]).then_inc(tables, 16)
            sp.dma_start(sj_dram.ap().rearrange("(t p) d -> p t d", p=P), g.sj[:]).then_inc(tables, 16)
            sp.wait_ge(tables, 48)

        @block.tensor
        def _(pe):
            pe.wait_ge(loaded, 48)
            with pe.Fori(0, T) as t:
                pe.wait_ge(staged, t + 1)
                for q in range(2):
                    last = nc.tensor.transpose(p_t[:, q, :], tile[:, q * P:(q + 1) * P], g.ident[:])
                last.then_inc(turn, 1)
                pe.wait_ge(back, t + 1)
                pe.wait_ge(copied, t + 1)
                for q in range(2):
                    last = nc.tensor.matmul(p_w[:, 0:D], turned[:, q, :], w[:, q, :], start=q == 0, stop=q == 1)
                last.then_inc(product, 1)

        @block.scalar
        def _(act):
            act.sem_inc(copied, 1)
            with act.Fori(0, T) as t:
                act.wait_ge(turn, t + 1)
                nc.scalar.copy(turned[:], p_t[:, 0:2, :]).then_inc(back, 1)
                act.wait_ge(product, t + 1)
                nc.scalar.copy(y[:, bass.ds(t, 1), :].rearrange("p t d -> p (t d)"), p_w[:, 0:D]).then_inc(copied, 1)
            roots.root(act, b["nb"][:], b["bb"][:])
            roots.root(act, s["nx"][:], s["xx"][:])
            act.wait_ge(logs_of["x"], 1)
            nc.scalar.activation(s["t1"][:], s["t1"][:], ACT.Ln).then_inc(lns, 1)
            roots.root(act, s["nw"][:], s["ww"][:])
            act.wait_ge(logs_of["u"], 1)
            nc.scalar.activation(s["t1"][:], s["nu"][:], ACT.Tanh).then_inc(tanhs, 1)
            nc.scalar.activation(b["t1"][:], b["nb"][:], ACT.Tanh).then_inc(tanhs, 1)
            roots.root(act, b["nb"][:], b["bb"][:])
            roots.root(act, s["nr"][:], s["rr"][:])
            act.wait_ge(logs_of["r"], 1)
            nc.scalar.activation(s["t1"][:], s["t1"][:], ACT.Ln).then_inc(lns, 1)

        @block.vector
        def _(dve):
            c = Count(dve, vec)
            v = Vector(nc, dve, c, roots)
            nc.vector.tensor_copy(tile[:], g.x[:, 0, :]).then_inc(staged, 1)
            with dve.Fori(1, T) as t:
                dve.wait_ge(turn, t)
                nc.vector.tensor_copy(tile[:], g.x[:, bass.ds(t, 1), :].rearrange("p t d -> p (t d)")
                                      ).then_inc(staged, 1)

            def clipped_root(out, x, t):
                v.sqrt(out, x, t)
                v.ts(out, out, 1e-15, ALU.max)

            def arctanh_over(out, n, which, t1, t2, t3, turn_no):
                y1 = out
                v.ts(y1, n, LARGEST, ALU.min)
                v.ts(t1, y1, -1.0, ALU.mult, 1.0, ALU.add)
                v.recip(t1, t1)
                v.ts(t2, y1, 1.0, ALU.add)
                v.tt(t1, t1, t2, ALU.mult)
                dve.sem_inc(logs_of[which], 1)
                v.tt(t2, y1, y1, ALU.mult)
                v.ts(t3, t2, 1.0 / 15, ALU.mult, 1.0 / 13, ALU.add)
                for k in (11, 9, 7, 5, 3, 1):
                    v.tt(t3, t3, t2, ALU.mult)
                    v.ts(t3, t3, 1.0 / k, ALU.add)
                v.recip(t2, n)
                v.tt(t3, t3, y1, ALU.mult)
                dve.wait_ge(lns, turn_no)
                v.ts(t1, t1, 0.5, ALU.mult)
                v.tt(t1, t1, t3, ALU.subtract)
                v.ts(y1, y1, 0.3, ALU.is_ge)
                v.tt(t1, t1, y1, ALU.mult)
                v.tt(t1, t1, t3, ALU.add)
                v.tt(out, t1, t2, ALU.mult)

            S = {n: t[:] for n, t in s.items()}
            B1 = {n: t[:] for n, t in b.items()}
            dve.wait_ge(loaded, 48)
            v.tt(tmp, g.x[:], g.x[:], ALU.mult)
            v.row_sum(S["xx"], tmp)
            v.tt(tmp[:, 0, :], hb[:], hb[:], ALU.mult)
            v.row_sum(B1["bb"], tmp[:, 0, :])
            clipped_root(B1["nb"], B1["bb"], B1["t1"])
            clipped_root(S["nx"], S["xx"], S["t1"])
            arctanh_over(S["fx"], S["nx"], "x", S["t1"], S["t2"], S["t3"], 1)
            dve.wait_ge(copied, T + 1)
            v.tt(tmp, y, y, ALU.mult)
            v.row_sum(S["ww"], tmp)
            v.sqrt(S["nw"], S["ww"], S["t1"])
            v.tt(S["nu"], S["nw"], S["fx"], ALU.mult)
            v.ts(S["nu"], S["nu"], 1e-15, ALU.max)
            dve.sem_inc(logs_of["u"], 1)
            v.recip(S["t2"], S["nu"])
            v.tt(S["t2"], S["t2"], S["fx"], ALU.mult)
            dve.wait_ge(tanhs, 2)
            v.tt(S["c"], S["t1"], S["t2"], ALU.mult)
            v.tt(S["t1"], S["c"], S["nw"], ALU.mult)
            v.ts(S["t1"], S["t1"], 1e-15, ALU.max)
            v.to_one(S["c"], S["t1"], MAXN, S["t2"])
            v.recip(B1["c"], B1["nb"])
            v.tt(B1["c"], B1["c"], B1["t1"], ALU.mult)
            v.ts(hb[:], hb[:], B1["c"], ALU.mult)
            v.tt(tmp[:, 0, :], hb[:], hb[:], ALU.mult)
            v.row_sum(B1["bb"], tmp[:, 0, :])
            clipped_root(B1["nb"], B1["bb"], B1["t1"])
            v.ts(B1["c"], B1["c"], 0.0, ALU.mult, 1.0, ALU.add)
            v.to_one(B1["c"], B1["nb"], MAXN, B1["t1"])
            v.ts(hb[:], hb[:], B1["c"], ALU.mult)
            v.tt(tmp[:, 0, :], hb[:], hb[:], ALU.mult)
            v.row_sum(B1["bb"], tmp[:, 0, :])
            v.tt(tmp, y, over_tiles(hb[:]), ALU.mult)
            v.row_sum(S["wb"], tmp)
            v.tt(S["t1"], S["c"], S["nw"], ALU.mult)
            v.tt(S["t1"], S["t1"], S["t1"], ALU.mult)
            v.tt(S["t2"], S["c"], S["wb"], ALU.mult)
            v.ts(S["t2"], S["t2"], 2.0, ALU.mult, 1.0, ALU.add)
            v.stt(S["t3"], S["t1"], B1["bb"], S["t2"], ALU.mult, ALU.add)
            v.ts(S["t3"], S["t3"], 1e-15, ALU.max)
            v.recip(S["t3"], S["t3"])
            v.stt(S["A"], S["t2"], B1["bb"], S["t3"], ALU.add, ALU.mult)
            v.tt(S["A"], S["A"], S["c"], ALU.mult)
            v.ts(S["t1"], S["t1"], -1.0, ALU.mult, 1.0, ALU.add)
            v.tt(S["B"], S["t1"], S["t3"], ALU.mult)
            v.tt(y, y, over_features(S["A"]), ALU.mult)
            v.tt(tmp, over_tiles(hb[:]), over_features(S["B"]), ALU.mult)
            v.tt(y, y, tmp, ALU.add)
            v.tt(tmp, y, y, ALU.mult)
            v.row_sum(S["rr"], tmp)
            clipped_root(S["nr"], S["rr"], S["t1"])
            v.ts(S["c"], S["nr"], 0.0, ALU.mult, 1.0, ALU.add)
            v.to_one(S["c"], S["nr"], MAXN, S["t1"])
            v.tt(S["nr"], S["nr"], S["c"], ALU.mult)
            v.ts(S["nr"], S["nr"], 1e-15, ALU.max)
            arctanh_over(S["fx"], S["nr"], "r", S["t1"], S["t2"], S["t3"], 2)
            v.tt(S["c"], S["c"], S["fx"], ALU.mult)
            v.tt(y, y, over_features(S["c"]), ALU.mult)
            dve.sem_inc(logs, 1)
            dve.wait_ge(lx_in, 128)
            y4 = y.rearrange("p t (h d) -> p t h d", h=H)
            tmp4 = tmp.rearrange("p t (h d) -> p t h d", h=H)
            for lo, out in ((0, g.si), (DH, g.sj)):
                for h in range(H):
                    v.tt(tmp4[:, :, h, :], y4[:, :, h, :], over_tiles(att[:, h, lo:lo + DH]), ALU.mult)
                v.row_sum(out[:].rearrange("p t h -> p (t h)"), tmp.rearrange("p t (h d) -> p (t h) d", h=H))
            dve.sem_inc(scored, 1)


def neighbour_max(nc, g, sj_dram):
    with ExitStack() as ctx:
        m = Mem(nc, ctx, "nmax")
        rows = m.sb("rows", [P, BODY, H])
        ring_row = m.sb("ring_row", [P, BODY], I32)
        away = m.sb("away", [P, 2 * GRP, P])
        four = m.sb("four", [P, H, P])
        best = m.sb("best", [P, T, H])
        tmp = m.sb("tmp", [P, T, H])
        p_t = m.ps("p_t", [P, 2, H, P])
        staged, tick, used, vec, copied, turn, reduced = (m.sem(n) for n in (
            "staged", "tick", "used", "vec", "copied", "turn", "reduced"))
        landed = [m.sem(f"landed_{r}") for r in range(RING)]
        block = ctx.enter_context(nc.Block())
        lane_max = g.big[:, 0:(T + 1) * H * P].rearrange("p (t h n) -> p t h n", h=H, n=P)

        @block.scalar
        def _(act):
            def stage(at, r):
                nc.scalar.copy(ring_row[:, r * GRP:(r + 1) * GRP],
                               g.rec[0][:, bass.ds(at, GRP), 0]).then_inc(staged, 1)

            for r in range(RING):
                stage(r * GRP, r)
            with act.Fori(1, LOOPS) as i:
                for r in range(RING):
                    act.wait_ge(used, i * RING + (r + 1 - RING))
                    stage(i * BODY + r * GRP, r)
            act.wait_ge(used, LOOPS * RING)
            act.sem_inc(turn, 1)
            with act.Fori(0, T) as t:
                act.wait_ge(turn, t + 1)
                nc.scalar.copy(four[:].rearrange("p h n -> p (h n)"),
                               lane_max[:, bass.ds(t, 1), :, :].rearrange("p t h n -> p (t h n)")).then_inc(copied, 1)

        @block.gpsimd
        def _(pool):
            with pool.Fori(0, LOOPS) as i:
                for r in range(RING):
                    pool.wait_ge(staged, i * RING + (r + 1))
                    pool.sem_inc(tick, 1)
                    for j in range(r * GRP, (r + 1) * GRP):
                        pool.indirect_dma_start(rows[:, j, :], None, sj_dram.ap(), bass.IndirectOffsetOnAxis(
                            ap=ring_row[:, j:j + 1], axis=0)).then_inc(landed[r], 16)

        @block.tensor
        def _(pe):
            with pe.Fori(0, T) as t:
                pe.wait_ge(copied, t + 1)
                pe.wait_ge(reduced, t + 1)
                for h in range(H):
                    last = nc.tensor.transpose(p_t[:, 0, h, :], four[:, h, :], g.ident[:])
                last.then_inc(turn, 1)

        @block.vector
        def _(dve):
            c = Count(dve, vec)
            v = Vector(nc, dve, c)
            v.did(nc.vector.memset(g.big[:, 0:(T + 1) * H * P], FAR))
            with dve.Fori(0, LOOPS) as i:
                c.enter(i, BODY * 2)
                for r in range(RING):
                    tiles = [dve.value_load(g.pair_tile[0][0:1, bass.ds(i * (BODY // 2) + (2 * r + q), 1)],
                                            min_val=0, max_val=T) for q in range(2)]
                    for q in range(GRP):
                        c.step(nc.vector.tensor_scalar(away[:, (r % 2) * GRP + q, :], g.iota[:, 0:P],
                                                       g.rec[0][:, bass.ds(i * BODY + (r * GRP + q), 1), 2], FAR,
                                                       ALU.not_equal, ALU.mult))
                    c.wait()
                    dve.wait_ge(landed[r], i * (16 * GRP) + 16 * GRP)
                    for q in range(GRP):
                        for h in range(H):
                            at = lane_max[:, bass.ds(tiles[q // 2], 1), h, :].rearrange("p t n -> p (t n)")
                            last = nc.vector.scalar_tensor_tensor(at, away[:, (r % 2) * GRP + q, :],
                                                                  rows[:, r * GRP + q, h:h + 1], at,
                                                                  ALU.add, ALU.max)
                        c.step(last)
                        c.wait()
                    dve.sem_inc(used, 1)
            c.leave(LOOPS)
            dve.sem_inc(reduced, 1)
            with dve.Fori(0, T) as t:
                dve.wait_ge(turn, t + 2)
                nc.vector.tensor_reduce(best[:, bass.ds(t, 1), :].rearrange("p t h -> p (t h)"), p_t[:, 0, :, :],
                                        AX.X, ALU.max).then_inc(reduced, 1)
            dve.wait_ge(reduced, T + 1)
            si, top = g.sm[:, 0:T, 0:H], g.sm[:, 0:T, H:2 * H]
            v.did(nc.vector.memset(g.sm[:], 0.0))
            v.did(nc.vector.tensor_copy(si, g.si[:]))
            v.tt(best[:], best[:], g.sj[:], ALU.max)
            v.tt(best[:], best[:], g.si[:], ALU.add)
            v.ts(tmp[:], best[:], 0.2, ALU.mult)
            v.tt(top, best[:], tmp[:], ALU.max)


def attend(nc, g, msg_dram):
    W = D + H
    with ExitStack() as ctx:
        m = Mem(nc, ctx, "att")
        rows = m.sb("rows", [P, BODY, W])
        weighted = m.sb("weighted", [P, 2 * GRP, W])
        hot = m.sb("hot", [P, BODY, P])
        hot_t = m.sb("hot_t", [P, 2, GRP, P])
        alpha = m.sb("alpha", [P, 2, GRP, H])
        slope = m.sb("slope", [P, GRP, H])
        ring_row = m.sb("ring_row", [P, BODY], I32)
        sums = m.ps("sums", [P, 4, 512])
        p_t = m.ps("p_t", [P, 2, GRP, P])
        p_s = m.ps("p_s", [P, 2, 512])
        (staged, tick, hot_ready, turn, back, looked, alphas, exps, ready, summed, added, vec, psum_free) = (
            m.sem(n) for n in ("staged", "tick", "hot_ready", "turn", "back", "looked", "alphas", "exps", "ready",
                               "summed", "added", "vec", "psum_free"))
        landed = [m.sem(f"landed_{r}") for r in range(RING)]
        block = ctx.enter_context(nc.Block())

        @block.gpsimd
        def _(pool):
            with pool.Fori(0, LOOPS) as i:
                for r in range(RING):
                    pool.wait_ge(staged, i * RING + (r + 1))
                    pool.sem_inc(tick, 1)
                    for j in range(r * GRP, (r + 1) * GRP):
                        pool.indirect_dma_start(rows[:, j, :], None, msg_dram.ap(), bass.IndirectOffsetOnAxis(
                            ap=ring_row[:, j:j + 1], axis=0)).then_inc(landed[r], 16)

        @block.scalar
        def _(act):
            def stage(at, r):
                nc.scalar.copy(ring_row[:, r * GRP:(r + 1) * GRP],
                               g.rec[0][:, bass.ds(at, GRP), 0]).then_inc(staged, 1)

            for r in range(RING):
                stage(r * GRP, r)

            def group(i, r, more):
                n = i * RING + (r + 1)
                act.wait_ge(turn, n)
                nc.scalar.copy(hot_t[:, r % 2, :, :], p_t[:, r % 2, :, :]).then_inc(back, 1)
                act.wait_ge(alphas, n)
                nc.scalar.activation(weighted[:, (r % 2) * GRP:(r % 2 + 1) * GRP, D:W], alpha[:, r % 2, :, :],
                                     ACT.Exp).then_inc(exps, 1)
                if more:
                    act.wait_ge(ready, n)
                    stage(i * BODY + (r * GRP + BODY), r)

            with act.Fori(0, LOOPS - 1) as i:
                for r in range(RING):
                    group(i, r, True)
            for r in range(RING):
                group(LOOPS - 1, r, False)

        @block.tensor
        def _(pe):
            with pe.Fori(0, LOOPS) as i:
                for r in range(RING):
                    n = i * RING + (r + 1)
                    tiles = [pe.value_load(g.pair_tile[0][0:1, bass.ds(i * (BODY // 2) + (2 * r + q), 1)],
                                           min_val=0, max_val=T) for q in range(2)]
                    pe.wait_ge(hot_ready, n)
                    for q in range(GRP):
                        last = nc.tensor.transpose(p_t[:, r % 2, q, :], hot[:, r * GRP + q, :], g.ident[:])
                    last.then_inc(turn, 1)
                    pe.wait_ge(back, n)
                    for q in range(GRP):
                        last = nc.tensor.matmul(p_s[:, r % 2, 8 * q:8 * q + 8], hot_t[:, r % 2, q, :],
                                                g.sm[:, bass.ds(tiles[q // 2], 1), :].rearrange("p t s -> p (t s)"),
                                                start=True, stop=True)
                    last.then_inc(looked, 1)
                    pe.wait_ge(ready, n)
                    pe.wait_ge(psum_free, n)
                    for q in range(GRP):
                        last = nc.tensor.matmul(sums[:, 2 * (r % 2) + q // 2, 0:W], hot[:, r * GRP + q, :],
                                                weighted[:, (r % 2) * GRP + q, :], start=q % 2 == 0, stop=q % 2 == 1)
                    last.then_inc(summed, 1)

        @block.vector
        def _(dve):
            c = Count(dve, vec)
            v = Vector(nc, dve, c)

            def build(at, r):
                for q in range(GRP):
                    last = nc.vector.tensor_scalar(hot[:, r * GRP + q, :], g.iota[:, 0:P],
                                                   g.rec[0][:, bass.ds(at + q, 1), 2], None, ALU.is_equal)
                last.then_inc(hot_ready, 1)

            dve.sem_inc(psum_free, 2)
            build(0, 0)
            with dve.Fori(0, LOOPS) as i:
                c.enter(i, RING * 4)
                for r in range(RING):
                    n = i * RING + (r + 1)
                    build(i * BODY + (r + 1) * GRP, (r + 1) % RING)
                    tiles = [dve.value_load(g.pair_tile[0][0:1, bass.ds(i * (BODY // 2) + (2 * r + q), 1)],
                                            min_val=0, max_val=T) for q in range(2)]
                    al = alpha[:, r % 2, :, :]
                    look = p_s[:, r % 2, 0:8 * GRP].rearrange("p (q s) -> p q s", s=8)
                    dve.wait_ge(landed[r], i * (16 * GRP) + 16 * GRP)
                    dve.wait_ge(looked, n)
                    v.tt(al, rows[:, r * GRP:(r + 1) * GRP, D:W], look[:, :, 0:H], ALU.add)
                    v.ts(slope[:], al, 0.2, ALU.mult)
                    v.tt(al, al, slope[:], ALU.max)
                    v.tt(al, al, look[:, :, H:2 * H], ALU.subtract)
                    dve.sem_inc(alphas, 1)
                    dve.wait_ge(exps, n)
                    for q in range(GRP):
                        wq = weighted[:, (r % 2) * GRP + q, :]
                        last = nc.vector.tensor_tensor(
                            wq[:, 0:D].rearrange("p (h d) -> p h d", h=H),
                            rows[:, r * GRP + q, 0:D].rearrange("p (h d) -> p h d", h=H),
                            wq[:, D:W].unsqueeze(2).broadcast_to([P, H, DH]), ALU.mult)
                    last.then_inc(ready, 1)
                    dve.wait_ge(summed, n)
                    for q in range(2):
                        if r + q:
                            dve.wait_ge(added, i * (2 * RING) + (2 * r + q))
                        at = g.acc[:, bass.ds(tiles[q], 1), 0:W].rearrange("p t d -> p (t d)")
                        nc.vector.tensor_tensor(at, sums[:, 2 * (r % 2) + q, 0:W], at, ALU.add).then_inc(added, 1)
                    dve.wait_ge(added, i * (2 * RING) + (2 * r + 2))
                    dve.sem_inc(psum_free, 1)
            c.leave(LOOPS)


def hyperbolic_finish(nc, g, a, msg_dram, o_dram):
    W = D + H
    with ExitStack() as ctx:
        m = Mem(nc, ctx, "fin")
        bias = m.sb("bias", [P, D])
        own = m.sb("own", [P, T, H])
        tmp_h = m.sb("tmp_h", [P, T, H])
        total = m.sb("total", [P, T, H])
        square, norm, scale, t1 = (m.sb(n, [P, T]) for n in ("square", "norm", "scale", "t1"))
        roots, ln = Roots(nc, m), NormTiles(m)
        loaded, alphas, exps, vec, divided, out_stored, out_in, norms, tanhs = (m.sem(n) for n in (
            "loaded", "alphas", "exps", "vec", "divided", "out_stored", "out_in", "norms", "tanhs"))
        block = ctx.enter_context(nc.Block())
        y, tmp = g.y, g.tmp
        flat = o_dram.ap().rearrange("n (q d) -> (n q) d", d=DH)

        @block.sync
        def _(sp):
            sp.dma_start(bias[:], row_of_all(a["L2_gnn_b_conv"])).then_inc(loaded, 16)
            sp.dma_start(y, msg_dram.ap()[:, 0:D].rearrange("(t p) d -> p t d", p=P)).then_inc(loaded, 16)
            sp.wait_ge(divided, 1)
            for h in range(H):
                sp.dma_start(flat[h * N:h * N + (T - 1) * P, :].rearrange("(t p) d -> p t d", p=P),
                             y[:, 0:T - 1, h * DH:(h + 1) * DH]).then_inc(out_stored, 16)
                sp.dma_start(flat[h * N + (T - 1) * P:(h + 1) * N, :],
                             y[0:LAST, T - 1, h * DH:(h + 1) * DH]).then_inc(out_stored, 16)
            sp.wait_ge(out_stored, 128)
            sp.dma_start(y[:, 0:T - 1, :], o_dram.ap()[0:(T - 1) * P, :].rearrange("(t p) d -> p t d", p=P)
                         ).then_inc(out_in, 16)
            sp.dma_start(y[0:LAST, T - 1, :], o_dram.ap()[(T - 1) * P:N, :]).then_inc(out_in, 16)

        @block.scalar
        def _(act):
            act.wait_ge(alphas, 1)
            nc.scalar.activation(own[:], own[:], ACT.Exp).then_inc(exps, 1)
            roots.root(act, norm[:], square[:])
            act.wait_ge(norms, 1)
            nc.scalar.activation(t1[:], norm[:], ACT.Tanh).then_inc(tanhs, 1)
            roots.root(act, ln.root[:], ln.var[:])

        @block.vector
        def _(dve):
            c = Count(dve, vec)
            v = Vector(nc, dve, c, roots)
            v.tt(own[:], g.si[:], g.sj[:], ALU.add)
            v.ts(tmp_h[:], own[:], 0.2, ALU.mult)
            v.tt(own[:], own[:], tmp_h[:], ALU.max)
            v.tt(own[:], own[:], g.sm[:, 0:T, H:2 * H], ALU.subtract)
            dve.sem_inc(alphas, 1)
            dve.wait_ge(exps, 1)
            dve.wait_ge(loaded, 32)
            v.tt(total[:], g.acc[:, 0:T, D:W], own[:], ALU.add)
            v.ts(total[:], total[:], 1e-15, ALU.max)
            v.recip(total[:], total[:])
            for h in range(H):
                cols = slice(h * DH, (h + 1) * DH)
                v.tt(y[:, :, cols], y[:, :, cols], over_features(own[:, :, h], DH), ALU.mult)
                v.tt(y[:, :, cols], y[:, :, cols], g.acc[:, 0:T, cols], ALU.add)
                v.tt(y[:, :, cols], y[:, :, cols], over_features(total[:, :, h], DH), ALU.mult)
            dve.sem_inc(divided, 1)
            dve.wait_ge(out_in, 32)
            v.tt(y, y, over_tiles(bias[:]), ALU.add)
            v.ts(y, y, 0.0, ALU.max)
            v.tt(tmp, y, y, ALU.mult)
            v.row_sum(square[:], tmp)
            v.sqrt(norm[:], square[:], t1[:])
            v.ts(norm[:], norm[:], 1e-15, ALU.max)
            dve.sem_inc(norms, 1)
            v.recip(scale[:], norm[:])
            dve.wait_ge(tanhs, 1)
            v.tt(scale[:], scale[:], t1[:], ALU.mult)
            v.tt(norm[:], norm[:], scale[:], ALU.mult)
            v.ts(norm[:], norm[:], 1e-15, ALU.max)
            v.to_one(scale[:], norm[:], MAXN, t1[:])
            v.tt(y, y, over_features(scale[:]), ALU.mult)
            v.tt(g.x[:], g.x[:], y, ALU.add)
            normalise(nc, g, ln, dve, c, v)


def build(nc, a, out):
    dram = lambda name, shape: nc.dram_tensor(name, shape, F32)
    h_dram = dram("batch_normed", (NP, D))
    t_dram = [dram(f"relation_rows_{n}", (NP * R, D)) for n in range(2)]
    lx_dram, o_dram = dram("log_rows", (NP, D)), dram("attended", (NP, D))
    msg_dram, sj_dram = dram("messages", (NP, D + H)), dram("scores", (NP, H))
    with ExitStack() as ctx:
        m = Mem(nc, ctx, "g")
        g = Shared()
        g.iota = m.sb("iota", [P, CHP])
        g.pair_start = m.sb("pair_start", [P, CHP // 2])
        g.ident = m.sb("ident", [P, P])
        g.minus_upto = m.sb("minus_upto", [P, P], BF16)
        g.ones_b = m.sb("ones_b", [P, P], BF16)
        g.ones_f = m.sb("ones_f", [P, P])
        g.rec = [m.sb(f"rec_{k}", [P, CHP, 4]) for k in range(2)]
        g.pair_tile = [m.sb(f"pair_tile_{k}", [P, CHP // 2], I32) for k in range(2)]
        make_constants(nc, g)
        sort_edges(nc, g, a["src"], a["dst"], a["edge_type_8"], a["edge_weight"], a["edge_weight_n2"])
        g.x = m.sb("x", [P, T, D])
        g.acc = m.sb("acc", [P, T + 1, D + H])
        g.si, g.sj = m.sb("si", [P, T, H]), m.sb("sj", [P, T, H])
        g.sm = m.sb("sm", [P, T + 1, 2 * H])
        g.big = m.sb("big", [P, (T + 1) * H * P])
        g.h = g.big[:, 0:T * D].rearrange("p (t d) -> p t d", d=D)
        g.acc2 = g.big[:, T * D:T * D + (T + 1) * (D + 1)].rearrange("p (t d) -> p t d", d=D + 1)
        g.y = g.h
        g.tmp = g.big[:, T * D:2 * T * D].rearrange("p (t d) -> p t d", d=D)
        load_and_batch_norm(nc, g, a, h_dram)
        aggregate(nc, g, "in", 0, h_dram.ap(), D, 0, g.acc, True, 1)
        aggregate(nc, g, "out", 1, h_dram.ap(), D, 0, g.acc2, True, 1)
        gated_update(nc, g, a)
        relation_tables(nc, g, a, "mix", t_dram[0], False)
        aggregate(nc, g, "rel1", 0, t_dram[0].ap(), D, 1, g.acc, False, 0)
        relu_update(nc, g, "relu1", a["L1_gnn_bias"])
        hyperbolic_prepare(nc, g, a, lx_dram, msg_dram, sj_dram)
        neighbour_max(nc, g, sj_dram)
        clear(nc, g)
        attend(nc, g, msg_dram)
        hyperbolic_finish(nc, g, a, msg_dram, o_dram)
        relation_tables(nc, g, a, "rel", t_dram[1], True)
        aggregate(nc, g, "rel3", 1, t_dram[1].ap(), D, 1, g.acc, False, 0)
        relu_update(nc, g, "relu3", a["L3_gnn_bias"], out=out)


def clear(nc, g):
    with ExitStack() as ctx:
        block = ctx.enter_context(nc.Block())

        @block.vector
        def _(dve):
            nc.vector.memset(g.acc[:], 0.0)


_TURNED = {"L0_gnn_W_in": "L0_gnn_W_in_T", "L0_gnn_W_out": "L0_gnn_W_out_T", "L2_gnn_W": "L2_gnn_W_T"}


def kernel(**inputs):
    import numpy as _np
    import concourse.bacc as _bacc
    from concourse import mybir as _mybir
    from concourse.bass_utils import run_bass_kernel_spmd as _run

    nc = _bacc.Bacc("TRN2", target_bir_lowering=False, num_devices=1)
    arrays, args = {}, {}
    for name, a in inputs.items():
        a = _np.asarray(a)
        name, a = (_TURNED[name], a.T) if name in _TURNED else (name, a)
        a = _np.ascontiguousarray(a)
        arrays[f"in_{name}"] = a
        args[name] = nc.dram_tensor(f"in_{name}", a.shape, _mybir.dt.from_np(a.dtype), kind="ExternalInput").ap()
    out = nc.dram_tensor("out_0", (N, D), F32, kind="ExternalOutput").ap()
    build(nc, args, out)
    return _run(nc, [arrays], core_ids=[0]).results[0]["out_0"]
```

```python
from contextlib import ExitStack

import numpy as np
import concourse.bass as bass
from concourse import mybir

F32 = mybir.dt.float32
BF16 = mybir.dt.bfloat16
I32 = mybir.dt.int32
I16 = mybir.dt.int16
ALU = mybir.AluOpType
ACT = mybir.ActivationFunctionType
AX = mybir.AxisListType

P = 128
N = 3125
E = 100000
D = 256
R = 8
NB = 4
H = 4
DH = D // H
T = -(-N // P)
NP = T * P
LAST = N - (T - 1) * P
BUCKETS = T + 1
GRP = 4
RING = 4
BODY = GRP * RING
EC = -(-E // (P * BODY)) * BODY
EH = EC // 2
PAIRS = -(-E // (2 * P)) + T
CH = -(-2 * PAIRS // BODY) * BODY
CHP = -(-(P * EC + BUCKETS * (2 * P - 1)) // (2 * P)) * 2 + GRP
LOOPS = CH // BODY
EPS = 1e-5
MAXN = 1.0 - 0.004
LARGEST = float(np.float32(1.0 - 1e-7))
STEP = 2.0 ** 100


class Count:

    def __init__(self, eng, sem):
        self.eng, self.sem, self.n, self.base, self.k = eng, sem, 0, None, 0

    def step(self, ins):
        ins.then_inc(self.sem, 1)
        if self.base is None:
            self.n += 1
        else:
            self.k += 1

    def value(self):
        return self.n if self.base is None else self.base + self.k

    def wait(self, but=0):
        self.eng.wait_ge(self.sem, self.value() - but)

    def enter(self, i, per):
        assert self.base is None or self.k == self.per, (self.k, self.per)
        self.base, self.k, self.per = i * per + self.n, 0, per

    def leave(self, count):
        assert self.k == self.per, (self.k, self.per)
        self.n, self.base = self.n + count * self.per, None


class Mem:

    def __init__(self, nc, ctx, tag):
        self.nc, self.ctx, self.tag, self.sems = nc, ctx, tag, []
        ctx.callback(self.clear)

    def clear(self):
        if self.sems:
            self.nc.clear_and_free_semaphores(self.sems)
            self.nc.all_engine_barrier()

    def sb(self, name, shape, dt=F32):
        return self.ctx.enter_context(self.nc.sbuf_tensor(f"{self.tag}_{name}", shape, dt))

    def ps(self, name, shape, dt=F32):
        return self.ctx.enter_context(self.nc.psum_tensor(f"{self.tag}_{name}", shape, dt))

    def sem(self, name):
        self.sems.append(self.nc.alloc_semaphore(f"{self.tag}_{name}"))
        return self.sems[-1]


class Shared:
    pass


def make_constants(nc, g):
    with ExitStack() as ctx:
        m = Mem(nc, ctx, "const")
        made = m.sem("made")
        nums = m.sb("nums", [P, CHP], I32)
        pair_nums = m.sb("pair_nums", [P, CHP // 2], I32)
        block = ctx.enter_context(nc.Block())

        @block.gpsimd
        def _(pool):
            nc.gpsimd.iota(nums[:], [[1, CHP]], base=0, channel_multiplier=0).then_inc(made, 1)
            nc.gpsimd.iota(pair_nums[:], [[2 * P, CHP // 2]], base=0, channel_multiplier=0).then_inc(made, 1)
            nc.gpsimd.memset(g.ident[:], 0.0).then_inc(made, 1)
            nc.gpsimd.memset(g.minus_upto[:], -1.0).then_inc(made, 1)
            nc.gpsimd.memset(g.ones_b[:], 1.0)
            nc.gpsimd.memset(g.ones_f[:], 1.0)
            pool.wait_ge(made, 4)
            nc.gpsimd.tensor_copy(g.iota[:], nums[:])
            nc.gpsimd.tensor_copy(g.pair_start[:], pair_nums[:])
            nc.gpsimd.tensor_copy(g.iota_b[:], nums[:, 0:P])
            nc.gpsimd.affine_select(out=g.ident[:], in_=g.ident[:], compare_op=ALU.not_equal, fill=1.0,
                                    base=0, pattern=[[-1, P]], channel_multiplier=1).then_inc(made, 1)
            pool.wait_ge(made, 5)
            nc.gpsimd.tensor_copy(g.ident_b[:], g.ident[:])
            nc.gpsimd.affine_select(out=g.minus_upto[:], in_=g.minus_upto[:], compare_op=ALU.is_ge, fill=0.0,
                                    base=0, pattern=[[-1, P]], channel_multiplier=1)


def sort_edges(nc, g, a, h_dram):
    src, dst, etype, w_in, w_out = (a[n] for n in ("src", "dst", "edge_type_8", "edge_weight", "edge_weight_n2"))
    rec_dram = [nc.dram_tensor(f"records_by_{k}", (P * CHP, 4), F32) for k in ("dst", "src")]
    with ExitStack() as ctx:
        m = Mem(nc, ctx, "sort")
        e_end = [m.sb("e_dst", [P, EC], I32), m.sb("e_src", [P, EC], I32)]
        e_type = m.sb("e_type", [P, EC], I32)
        e_w = [m.sb("e_w_in", [P, EC]), m.sb("e_w_out", [P, EC])]
        empty = g.tmp.rearrange("p t d -> p (t d)")[:, 0:CHP * 4].rearrange("p (c w) -> p c w", w=4)
        records = [g.acc[:].rearrange("p t d -> p (t d)")[:, k * EC * 4:(k + 1) * EC * 4]
                   .rearrange("p (c w) -> p c w", w=4) for k in range(2)]
        place = [m.sb(f"place_{k}", [P, EC], I32) for k in range(2)]
        tile_no = m.sb("tile_no", [P, EC], I32)
        local = m.sb("local", [P, EC], I32)
        hot = m.sb("hot", [P, EC], BF16)
        zeros = m.sb("zeros", [P, EH])
        running = m.sb("running", [P, EC])
        rank = m.sb("rank", [P, EC])
        pos = m.sb("pos", [P, EC])
        pos_i = m.sb("pos_i", [P, EC], I32)
        base = m.sb("base", [P, 1])
        end_i = m.sb("end_i", [P, 2], I32)
        tile_count = m.sb("tile_count", [P, CHP // 2])
        ring_rec = m.sb("ring_rec", [P, BODY, 4])
        ring_place = m.sb("ring_place", [P, BODY], I32)
        before = m.ps("before", [P, 2, 512])
        total = m.ps("total", [P, 2, 512])

        filled = m.sem("filled")
        edges_in = m.sem("edges_in")
        emptied = m.sem("emptied")
        hot_ready = m.sem("hot_ready")
        ranked = m.sem("ranked")
        vec_step = m.sem("vec_step")
        placed = m.sem("placed")
        staged = m.sem("staged")
        tick = m.sem("tick")
        landed = [m.sem(f"landed_{r}") for r in range(RING)]
        rec_in = m.sem("rec_in")
        gamma, beta, mean, rstd, var, tmp = (m.sb(n, [P, D]) for n in ("gamma", "beta", "mean", "rstd", "var", "tmp"))
        ones_last = m.sb("ones_last", [P, P])
        p_mean = m.ps("p_mean", [P, 2, 512])
        x_in, masked, summed, squared, h_ready, h_out = (m.sem(n) for n in (
            "x_in", "masked", "summed", "squared", "h_ready", "h_out"))
        roots = Roots(nc, m)
        block = ctx.enter_context(nc.Block())

        full = P - 1
        rest = E - full * EC
        steps = EC // BODY

        @block.sync
        def _(sp):
            sp.wait_ge(filled, 1)
            for tile, arr in ((e_end[0], dst), (e_end[1], src), (e_type, etype), (e_w[0], w_in), (e_w[1], w_out)):
                sp.dma_start(tile[0:full, :], arr[0:full * EC].rearrange("(p c) -> p c", c=EC)).then_inc(edges_in, 16)
                sp.dma_start(tile[full:P, 0:rest], arr[full * EC:E].rearrange("(p c) -> p c", p=1)).then_inc(edges_in, 16)
            sp.wait_ge(filled, 2)
            for k in range(2):
                sp.dma_start(rec_dram[k].ap().rearrange("(p c) w -> p (c w)", p=P),
                             empty.rearrange("p c w -> p (c w)")).then_inc(emptied, 16)
            sp.dma_start(g.x[:, 0:T - 1, :],
                         a["x"][0:(T - 1) * P, :].rearrange("(t p) d -> p t d", p=P)).then_inc(x_in, 16)
            sp.dma_start(g.x[0:LAST, T - 1, :], a["x"][(T - 1) * P:N, :]).then_inc(x_in, 16)
            sp.dma_start(gamma[:], row_of_all(a["L0_gnn_gamma"])).then_inc(x_in, 16)
            sp.dma_start(beta[:], row_of_all(a["L0_gnn_beta"])).then_inc(x_in, 16)
            sp.wait_ge(h_ready, 1)
            sp.dma_start(h_dram.ap().rearrange("(t p) d -> p t d", p=P), g.h).then_inc(h_out, 16)
            for k in range(2):
                for r in range(RING):
                    sp.wait_ge(landed[r], 16 * GRP * steps * (k + 1))
                sp.dma_start(g.rec[k][:].rearrange("p c w -> p (c w)"),
                             rec_dram[k].ap().rearrange("(p c) w -> p (c w)", p=P)).then_inc(rec_in, 16)
            sp.wait_ge(rec_in, 32)
            sp.wait_ge(h_out, 16)

        @block.vector
        def _(dve):
            nc.vector.memset(e_end[0][:], NP)
            nc.vector.memset(e_end[1][:], NP)
            nc.vector.memset(e_type[:], 0)
            nc.vector.memset(e_w[0][:], 0.0)
            nc.vector.memset(e_w[1][:], 0.0).then_inc(filled, 1)
            c = Count(dve, vec_step)
            nc.vector.memset(g.x[:, T - 1, :], 0.0)
            c.step(nc.vector.memset(empty, 0.0))
            c.wait()
            nc.vector.memset(empty[:, :, 2], -1.0).then_inc(filled, 1)
            nc.vector.memset(zeros[:], 0.0)
            dve.wait_ge(edges_in, 160)
            for k in range(2):
                key, other, rec = e_end[k], e_end[1 - k], records[k]
                nc.vector.memset(tile_count[:], 0.0)
                nc.vector.memset(base[:], 0.0)
                nc.vector.memset(pos[:], 0.0)
                nc.vector.tensor_scalar(tile_no[:], key[:], 7, None, ALU.arith_shift_right)
                nc.vector.tensor_scalar(local[:], key[:], P - 1, None, ALU.bitwise_and)
                nc.vector.tensor_scalar(rec[:, :, 0], other[:], float(N - 1), None, ALU.min)
                nc.vector.tensor_copy(rec[:, :, 3], e_w[k][:])
                c.step(nc.vector.scalar_tensor_tensor(rank[:], other[:], float(R), e_type[:], ALU.mult, ALU.add))
                c.wait()
                nc.vector.tensor_copy(rec[:, :, 2], local[:])
                c.step(nc.vector.tensor_scalar(rec[:, :, 1], rank[:], float(N * R - 1), None, ALU.min))
                c.wait()
                with dve.Fori(0, BUCKETS) as b:
                    c.enter(b, 8)
                    nc.vector.tensor_scalar(hot[:], tile_no[:], g.iota[:, bass.ds(b, 1)], None,
                                            ALU.is_equal).then_inc(hot_ready, 1)
                    dve.wait_ge(ranked, b + (1 + BUCKETS * k))
                    for h in range(2):
                        c.step(nc.vector.tensor_tensor_scan(
                            running[:, h * EH:(h + 1) * EH], total[:, h, 0:EH], zeros[:],
                            base[:] if h == 0 else running[:, EH - 1:EH], ALU.add, ALU.max))
                        c.wait()
                    c.step(nc.vector.tensor_tensor(rank[:].rearrange("p (h c) -> p h c", h=2),
                                                   running[:].rearrange("p (h c) -> p h c", h=2),
                                                   before[:, :, 0:EH], ALU.add))
                    c.step(nc.vector.tensor_scalar(end_i[:, 0:1], running[:, EC - 1:EC], float(2 * P - 1), None,
                                                   ALU.add))
                    c.wait()
                    c.step(nc.vector.tensor_scalar(end_i[:, 1:2], end_i[:, 0:1], 8, 8, ALU.arith_shift_right,
                                                   ALU.arith_shift_left))
                    c.wait()
                    nc.vector.tensor_copy(base[:], end_i[:, 1:2])
                    c.step(nc.vector.copy_predicated(pos[:], hot[:].bitcast(I16), rank[:]))
                    c.wait()
                    c.step(nc.vector.scalar_tensor_tensor(tile_count[:], g.pair_start[:], base[:], tile_count[:],
                                                          ALU.is_ge, ALU.add))
                    c.wait()
                    c.step(nc.vector.tensor_copy(end_i[:, 0:1], end_i[:, 1:2]))
                c.leave(BUCKETS)
                nc.vector.tensor_scalar(g.pair_tile[k][:], tile_count[:], float(T), None, ALU.min)
                c.step(nc.vector.tensor_copy(pos_i[:], pos[:]))
                c.wait()
                nc.vector.tensor_scalar(tile_no[:], pos_i[:], 7, None, ALU.arith_shift_right)
                c.step(nc.vector.tensor_scalar(local[:], pos_i[:], P - 1, None, ALU.bitwise_and))
                c.wait()
                c.step(nc.vector.scalar_tensor_tensor(place[k][:], local[:], float(CHP), tile_no[:], ALU.mult,
                                                      ALU.add))
                c.wait()
                dve.sem_inc(placed, 1)
            v = Vector(nc, dve, c, roots)
            dve.wait_ge(summed, 1)
            v.ts(mean[:], p_mean[:, 0, 0:D], 1.0 / N, ALU.mult)
            v.tt(g.h, g.x[:], over_tiles(mean[:]), ALU.subtract)
            dve.wait_ge(emptied, 32)
            nc.vector.tensor_tensor(g.tmp, g.h, g.h, ALU.mult).then_inc(squared, 1)
            dve.wait_ge(summed, 2)
            v.ts(var[:], p_mean[:, 1, 0:D], 1.0 / N, ALU.mult, EPS, ALU.add)
            v.sqrt(rstd[:], var[:], tmp[:])
            v.recip(rstd[:], rstd[:])
            v.tt(rstd[:], rstd[:], gamma[:], ALU.mult)
            v.tt(g.h, g.h, over_tiles(rstd[:]), ALU.mult)
            v.tt(g.h, g.h, over_tiles(beta[:]), ALU.add)
            dve.sem_inc(h_ready, 1)

        @block.tensor
        def _(pe):
            for k in range(2):
                with pe.Fori(0, BUCKETS) as b:
                    pe.wait_ge(hot_ready, b + (1 + BUCKETS * k))
                    for h in range(2):
                        nc.tensor.matmul(before[:, h, 0:EH], g.minus_upto[:], hot[:, h * EH:(h + 1) * EH],
                                         start=True, stop=True)
                    for h in range(2):
                        last = nc.tensor.matmul(total[:, h, 0:EH], g.ones_b[:], hot[:, h * EH:(h + 1) * EH],
                                                start=True, stop=True)
                    last.then_inc(ranked, 1)
            pe.wait_ge(x_in, 64)
            for t in range(T):
                last = nc.tensor.matmul(p_mean[:, 0, 0:D], g.ones_f[:], g.x[:, t, :], start=t == 0, stop=t == T - 1)
            last.then_inc(summed, 1)
            pe.wait_ge(masked, 2)
            pe.wait_ge(squared, 1)
            for t in range(T):
                last = nc.tensor.matmul(p_mean[:, 1, 0:D], ones_last[:] if t == T - 1 else g.ones_f[:],
                                        g.tmp[:, t, :], start=t == 0, stop=t == T - 1)
            last.then_inc(summed, 1)

        @block.scalar
        def _(act):
            def stage(k, at, r):
                s = slice(r * GRP, (r + 1) * GRP)
                nc.scalar.copy(ring_place[:, s], place[k][:, bass.ds(at, GRP)])
                nc.scalar.copy(ring_rec[:, s, :], records[k][:, bass.ds(at, GRP), :]).then_inc(staged, 1)

            for k in range(2):
                act.wait_ge(placed, k + 1)
                if k:
                    roots.root(act, rstd[:], var[:])
                for r in range(RING):
                    if k:
                        act.wait_ge(landed[r], 16 * GRP * steps)
                    stage(k, r * GRP, r)
                with act.Fori(1, steps) as i:
                    for r in range(RING):
                        act.wait_ge(landed[r], i * (16 * GRP) + 16 * GRP * steps * k)
                        stage(k, i * BODY + r * GRP, r)

        @block.gpsimd
        def _(pool):
            nc.gpsimd.memset(ones_last[:], 1.0).then_inc(masked, 1)
            pool.wait_ge(masked, 1)
            nc.gpsimd.affine_select(out=ones_last[:], in_=ones_last[:], compare_op=ALU.is_gt, fill=0.0,
                                    base=LAST, pattern=[[0, P]], channel_multiplier=-1).then_inc(masked, 1)
            pool.wait_ge(emptied, 32)
            for k in range(2):
                with pool.Fori(0, steps) as i:
                    for r in range(RING):
                        pool.wait_ge(staged, i * RING + (r + 1 + RING * steps * k))
                        pool.sem_inc(tick, 1)
                        for j in range(r * GRP, (r + 1) * GRP):
                            pool.indirect_dma_start(rec_dram[k].ap(), bass.IndirectOffsetOnAxis(
                                ap=ring_place[:, j:j + 1], axis=0), ring_rec[:, j, :], None).then_inc(landed[r], 16)


def aggregate(nc, g, tag, k, table, words, word, acc, weighted, ones_column):
    width = words + ones_column
    with ExitStack() as ctx:
        m = Mem(nc, ctx, tag)
        rows = m.sb("rows", [P, BODY, width])
        hot = m.sb("hot", [P, BODY, P])
        ring_row = m.sb("ring_row", [P, BODY], I32)
        sums = m.ps("sums", [P, 2 * RING, 512])
        ready = m.sem("ready")
        staged = m.sem("staged")
        tick = m.sem("tick")
        hot_ready = m.sem("hot_ready")
        summed = m.sem("summed")
        psum_free = m.sem("psum_free")
        added = m.sem("added")
        landed = [m.sem(f"landed_{r}") for r in range(RING)]
        block = ctx.enter_context(nc.Block())

        @block.scalar
        def _(act):
            def stage(at, r):
                nc.scalar.copy(ring_row[:, r * GRP:(r + 1) * GRP],
                               g.rec[k][:, bass.ds(at, GRP), word]).then_inc(staged, 1)

            for r in range(RING):
                stage(r * GRP, r)
            with act.Fori(1, LOOPS) as i:
                for r in range(RING):
                    act.wait_ge(summed, i * RING + (r + 1 - RING))
                    stage(i * BODY + r * GRP, r)

        @block.gpsimd
        def _(pool):
            if ones_column:
                nc.gpsimd.memset(rows[:, :, words:width], 1.0).then_inc(ready, 1)
            with pool.Fori(0, LOOPS) as i:
                for r in range(RING):
                    pool.wait_ge(staged, i * RING + (r + 1))
                    pool.sem_inc(tick, 1)
                    for j in range(r * GRP, (r + 1) * GRP):
                        pool.indirect_dma_start(rows[:, j, 0:words], None, table, bass.IndirectOffsetOnAxis(
                            ap=ring_row[:, j:j + 1], axis=0)).then_inc(landed[r], 16)

        @block.tensor
        def _(pe):
            if ones_column:
                pe.wait_ge(ready, 1)
            with pe.Fori(0, LOOPS) as i:
                for r in range(RING):
                    pe.wait_ge(landed[r], i * (16 * GRP) + 16 * GRP)
                    pe.wait_ge(hot_ready, i * RING + (r + 1))
                    pe.wait_ge(psum_free, i * RING + (r + 1))
                    for q in range(GRP):
                        j = r * GRP + q
                        last = nc.tensor.matmul(sums[:, 2 * r + q // 2, 0:width], hot[:, j, :], rows[:, j, :],
                                                start=q % 2 == 0, stop=q % 2 == 1)
                    last.then_inc(summed, 1)

        @block.vector
        def _(dve):
            def build(at, r):
                for q in range(GRP):
                    last = nc.vector.tensor_scalar(
                        hot[:, r * GRP + q, :], g.iota[:, 0:P], g.rec[k][:, bass.ds(at + q, 1), 2],
                        g.rec[k][:, bass.ds(at + q, 1), 3] if weighted else None,
                        ALU.is_equal, ALU.mult if weighted else ALU.bypass)
                last.then_inc(hot_ready, 1)

            dve.sem_inc(psum_free, RING)
            build(0, 0)
            with dve.Fori(0, LOOPS) as i:
                tiles = tiles_of(nc, mybir.EngineType.DVE, g.pair_tile[k], i * (BODY // 2), BODY // 2)
                for r in range(RING):
                    build(i * BODY + (r + 1) * GRP, (r + 1) % RING)
                    dve.wait_ge(summed, i * RING + (r + 1))
                    for q in range(2):
                        if r + q:
                            dve.wait_ge(added, i * (2 * RING) + (2 * r + q))
                        at = acc[:, bass.ds(tiles[2 * r + q], 1), 0:width].rearrange("p t d -> p (t d)")
                        last = nc.vector.tensor_tensor(at, sums[:, 2 * r + q, 0:width], at, ALU.add)
                        last.then_inc(added, 1)
                    dve.wait_ge(added, i * (2 * RING) + (2 * r + 2))
                    dve.sem_inc(psum_free, 1)


class Vector:

    def __init__(self, nc, dve, count, roots=None):
        self.nc, self.dve, self.c, self.roots, self.asked = nc, dve, count, roots, 0

    def did(self, ins):
        self.c.step(ins)
        self.c.wait()

    def ts(self, out, x, s0, op0, s1=None, op1=ALU.bypass):
        self.did(self.nc.vector.tensor_scalar(out, x, s0, s1, op0, op1))

    def tt(self, out, x, y, op):
        self.did(self.nc.vector.tensor_tensor(out, x, y, op))

    def stt(self, out, x, s, y, op0, op1):
        self.did(self.nc.vector.scalar_tensor_tensor(out, x, s, y, op0, op1))

    def recip(self, out, x):
        self.did(self.nc.vector.reciprocal(out, x))

    def row_sum(self, out, x):
        self.did(self.nc.vector.tensor_reduce(out, x, AX.X, ALU.add))

    def sqrt(self, out, x, tmp):
        self.asked += 1
        self.dve.sem_inc(self.roots.asked, 1)
        self.dve.wait_ge(self.roots.given, self.asked)
        self.ts(out, out, 1e-30, ALU.max)
        self.recip(tmp, out)
        self.tt(tmp, tmp, x, ALU.mult)
        self.tt(out, out, tmp, ALU.add)
        self.ts(out, out, 0.5, ALU.mult)

    def to_one(self, scale, norm, most, tmp):
        self.recip(tmp, norm)
        self.ts(tmp, tmp, most, ALU.mult, 1.0, ALU.min)
        self.tt(scale, scale, tmp, ALU.mult)


class Roots:

    def __init__(self, nc, m):
        self.nc, self.asked, self.given, self.k = nc, m.sem("root_asked"), m.sem("root_given"), 0

    def root(self, act, out, x):
        self.k += 1
        act.wait_ge(self.asked, self.k)
        self.nc.scalar.activation(out, x, ACT.Sqrt).then_inc(self.given, 1)


class NormTiles:
    def __init__(self, m):
        self.stats = m.sb("stats", [P, T, 6])
        self.mean, self.var, self.tmp, self.root = (m.sb(n, [P, T]) for n in ("ln_mean", "ln_var", "ln_tmp", "ln_root"))


def in_pairs(eng, count, body):
    with eng.Fori(0, count // 2) as u:
        body(u * 2, 0)
        body(u * 2 + 1, 1)
    if count % 2:
        body(count - 1, (count - 1) % 2)


def in_turns(eng, body):
    body(0)
    with eng.Fori(1, LOOPS - 1) as i:
        body(i)
    body(LOOPS - 1)


def tiles_of(nc, engine, pair_tile, first, count):
    return nc.values_load_multi_w_load_instructions(
        pair_tile[0:1, bass.ds(first, count)], engines=[engine], min_val=0, max_val=T,
        skip_runtime_bounds_check_because="sort_edges counts them up from 0 and cuts them off at T")[1]


def row_of_all(ap):
    return ap.partition_broadcast(P)


def over_tiles(ap):
    return ap.unsqueeze(1).broadcast_to([P, T, ap.shape[1]])


def over_features(ap, n=D):
    return ap.unsqueeze(2).broadcast_to([*ap.shape, n])


def normalise(nc, g, ln, dve, c, v):
    stats, mean, var, tmp = ln.stats, ln.mean, ln.var, ln.tmp
    with dve.Fori(0, T) as t:
        c.enter(t, 1)
        c.step(nc.vector.bn_stats(stats[:, bass.ds(t, 1), :].rearrange("p t s -> p (t s)"),
                                  g.x[:, bass.ds(t, 1), :].rearrange("p t d -> p (t d)")))
    c.leave(T)
    c.wait()
    v.tt(mean[:], stats[:, :, 1], stats[:, :, 4], ALU.add)
    v.tt(tmp[:], stats[:, :, 1], stats[:, :, 4], ALU.subtract)
    v.tt(var[:], stats[:, :, 2], stats[:, :, 5], ALU.add)
    v.tt(tmp[:], tmp[:], tmp[:], ALU.mult)
    v.stt(var[:], tmp[:], float(D) / 4, var[:], ALU.mult, ALU.add)
    v.ts(mean[:], mean[:], 0.5, ALU.mult)
    v.ts(var[:], var[:], 1.0 / D, ALU.mult, EPS, ALU.add)
    v.sqrt(ln.root[:], var[:], tmp[:])
    v.recip(var[:], ln.root[:])
    v.tt(g.x[:], g.x[:], over_features(mean[:]), ALU.subtract)
    v.tt(g.x[:], g.x[:], over_features(var[:]), ALU.mult)


def gated_update(nc, g, a):
    with ExitStack() as ctx:
        m = Mem(nc, ctx, "gate")
        w_first = m.sb("w_first", [P, 2, 2, D])
        w_x = m.sb("w_x", [P, 4, 2 * D])
        w_all = m.sb("w_all", [P, 6, 2 * D])
        b_cols = m.sb("b_cols", [P, 4, 3])
        unit = m.sb("unit", [1, 3])
        b_x = m.sb("b_x", [1, 2 * D])
        b_all = m.sb("b_all", [3, 2 * D])
        tile = m.sb("tile", [P, 2, 3, D])
        sides = m.sb("sides", [P, T, 3])
        side = m.sb("side", [P, 2, 3])
        turned = m.sb("turned", [P, 2, 6, P])
        side_t = m.sb("side_t", [3, 2, P])
        gate = m.sb("gate", [P, 2, 2, D])
        tmp = m.sb("tmp", [P, D])
        roots, ln = Roots(nc, m), NormTiles(m)
        p_w = m.ps("p_w", [P, 512])
        p_t = m.ps("p_t", [P, 2, 8, P])
        p_g = m.ps("p_g", [P, 2, 512])
        cleared, loaded, product, copied, staged, turn, back, gates, acted, vec, done = (m.sem(n) for n in (
            "cleared", "loaded", "product", "copied", "staged", "turn", "back", "gates", "acted", "vec", "done"))
        block = ctx.enter_context(nc.Block())

        @block.sync
        def _(sp):
            sp.wait_ge(cleared, 1)
            for n, w in enumerate(("L0_gnn_W_in_T", "L0_gnn_W_out_T")):
                sp.dma_start(w_first[:, n, :, :], a[w].rearrange("(s p) i -> p s i", p=P)).then_inc(loaded, 16)
            sp.dma_start(w_x[:], a["L0_gnn_W_x2i"].rearrange("(s p) i -> p s i", p=P)).then_inc(loaded, 16)
            sp.dma_start(w_all[:, 4:6, :], a["L0_gnn_W_h2h"].rearrange("(s p) i -> p s i", p=P)).then_inc(loaded, 16)
            for n, b in enumerate(("L0_gnn_b_in", "L0_gnn_b_out")):
                for s in range(2):
                    sp.dma_start(b_cols[:, 2 * n + s, n:n + 1],
                                 a[b][s * P:(s + 1) * P].rearrange("(p a) -> p a", a=1)).then_inc(loaded, 16)
            sp.dma_start(b_x[:], a["L0_gnn_b_x2i"].rearrange("(a d) -> a d", a=1)).then_inc(loaded, 16)

        @block.tensor
        def _(pe):
            pe.wait_ge(loaded, 144)
            for n in range(2):
                for i in range(2):
                    if n + i:
                        pe.wait_ge(copied, 2 * n + i)
                    for s in range(2):
                        last = nc.tensor.matmul(p_w[:], w_first[:, n, s, i * P:(i + 1) * P], w_x[:, 2 * n + s, :],
                                                start=s == 0, stop=s == 1)
                    last.then_inc(product, 1)
            for s in range(4):
                nc.tensor.matmul(p_g[0:3, 0, :], b_cols[:, s, :], w_x[:, s, :], start=s == 0, stop=False)
            nc.tensor.matmul(p_g[0:3, 0, :], unit[:], b_x[:], start=False, stop=True).then_inc(product, 1)
            pe.wait_ge(copied, 5)
            def transposes(t, b):
                pe.wait_ge(staged, t * 4 + 4)
                for s in range(6):
                    nc.tensor.transpose(p_t[:, b, s, :], tile[:, b, s // 2, (s % 2) * P:(s % 2 + 1) * P], g.ident[:])
                nc.tensor.transpose(p_t[0:3, b, 6, :], side[:, b, :], g.ident[:]).then_inc(turn, 1)

            def products(t, b):
                pe.wait_ge(back, t * 3 + 3)
                pe.wait_ge(acted, t + 1)
                for s in range(6):
                    nc.tensor.matmul(p_g[:, b, :], turned[:, b, s, :], w_all[:, s, :], start=s == 0, stop=False)
                nc.tensor.matmul(p_g[:, b, :], side_t[:, b, :], b_all[:], start=False, stop=True).then_inc(gates, 1)

            def step(t, b):
                transposes(t + 1, 1 - b)
                products(t, b)

            transposes(0, 0)
            in_pairs(pe, T - 1, step)
            products(T - 1, (T - 1) % 2)

        @block.scalar
        def _(act):
            act.sem_inc(acted, 2)

            def stage(t, b):
                nc.scalar.copy(tile[:, b, 0, :], g.acc[:, bass.ds(t, 1), 0:D].rearrange("p t d -> p (t d)")).then_inc(staged, 1)
                nc.scalar.copy(tile[:, b, 1, :], g.acc2[:, bass.ds(t, 1), 0:D].rearrange("p t d -> p (t d)")).then_inc(staged, 1)

            def back_of(t, b):
                act.wait_ge(turn, t + 1)
                nc.scalar.copy(turned[:, b, 0:4, :], p_t[:, b, 0:4, :]).then_inc(back, 1)

            def tanhs(t, b):
                act.wait_ge(gates, t + 1)
                act.wait_ge(done, t + 1)
                nc.scalar.activation(gate[:, b, 0, :], p_g[:, b, 0:D], ACT.Tanh, scale=0.5)
                nc.scalar.activation(gate[:, b, 1, :], p_g[:, b, D:2 * D], ACT.Tanh).then_inc(acted, 1)

            def step(t, b):
                back_of(t + 1, 1 - b)
                stage(t + 2, b)
                tanhs(t, b)

            stage(0, 0)
            back_of(0, 0)
            stage(1, 1)
            in_pairs(act, T - 2, step)
            back_of(T - 1, (T - 1) % 2)
            tanhs(T - 2, (T - 2) % 2)
            tanhs(T - 1, (T - 1) % 2)
            roots.root(act, ln.root[:], ln.var[:])

        @block.vector
        def _(dve):
            c = Count(dve, vec)
            v = Vector(nc, dve, c, roots)
            nc.vector.memset(b_cols[:], 0.0)
            nc.vector.memset(unit[:], 0.0)
            v.did(nc.vector.memset(sides[:, :, 2], 1.0))
            nc.vector.memset(unit[:, 2:3], 1.0).then_inc(cleared, 1)
            nc.vector.tensor_copy(sides[:, :, 0], g.acc[:, 0:T, D])
            v.did(nc.vector.tensor_copy(sides[:, :, 1], g.acc2[:, 0:T, D]))
            dve.sem_inc(done, 2)
            for s in range(4):
                dve.wait_ge(product, s + 1)
                nc.vector.tensor_copy(w_all[:, s, :], p_w[:]).then_inc(copied, 1)
            dve.wait_ge(product, 5)
            nc.vector.tensor_copy(b_all[:], p_g[0:3, 0, :]).then_inc(copied, 1)

            def stage(t, b):
                nc.vector.tensor_copy(side[:, b, :], sides[:, bass.ds(t, 1), :].rearrange("p t d -> p (t d)")).then_inc(staged, 1)
                nc.vector.tensor_copy(tile[:, b, 2, :], g.h[:, bass.ds(t, 1), :].rearrange("p t d -> p (t d)")).then_inc(staged, 1)

            def back_of(t, b):
                dve.wait_ge(turn, t + 1)
                nc.vector.tensor_copy(side_t[:, b, :], p_t[0:3, b, 6, :]).then_inc(back, 1)
                nc.vector.tensor_copy(turned[:, b, 4:6, :], p_t[:, b, 4:6, :]).then_inc(back, 1)

            def update(t, b):
                c.enter(t, 5)
                x = g.x[:, bass.ds(t, 1), :].rearrange("p t d -> p (t d)")
                dve.wait_ge(acted, t + 3)
                v.tt(tmp[:], g.h[:, bass.ds(t, 1), :].rearrange("p t d -> p (t d)"), gate[:, b, 1, :], ALU.subtract)
                v.ts(gate[:, b, 0, :], gate[:, b, 0, :], 0.5, ALU.mult, 0.5, ALU.add)
                v.tt(tmp[:], tmp[:], gate[:, b, 0, :], ALU.mult)
                v.tt(tmp[:], tmp[:], gate[:, b, 1, :], ALU.add)
                v.tt(x, x, tmp[:], ALU.add)
                dve.sem_inc(done, 1)

            def step(t, b):
                back_of(t + 1, 1 - b)
                stage(t + 2, b)
                update(t, b)

            stage(0, 0)
            back_of(0, 0)
            stage(1, 1)
            in_pairs(dve, T - 2, step)
            back_of(T - 1, (T - 1) % 2)
            update(T - 2, (T - 2) % 2)
            update(T - 1, (T - 1) % 2)
            c.leave(T)
            normalise(nc, g, ln, dve, c, v)


def relation_tables(nc, g, a, tag, t_dram, relational):
    parts = 2 if relational else 1
    with ExitStack() as ctx:
        m = Mem(nc, ctx, tag)
        w = m.sb("w", [P, parts, R, D])
        mix = m.sb("mix", [P, 2, P])
        comp = m.sb("comp", [P, NB])
        tile = m.sb("tile", [P, D])
        turned = m.sb("turned", [P, 2, P])
        mixed = m.sb("mixed", [P, P])
        table = m.sb("table", [P, 2, R, D])
        p_t = m.ps("p_t", [P, 2, P])
        p_m = m.ps("p_m", [P, P])
        p_o = m.ps("p_o", [P, 4, 2, D])
        loaded, made, staged, turn, back, mixing, unmixed, product, low_out, high_out = (m.sem(n) for n in (
            "loaded", "made", "staged", "turn", "back", "mixing", "unmixed", "product", "low_out", "high_out"))
        stored = [m.sem(f"stored_{q}") for q in range(2)]
        loads = 16 * (2 if relational else 1 + P // R)
        block = ctx.enter_context(nc.Block())

        @block.sync
        def _(sp):
            if relational:
                for s in range(2):
                    sp.dma_start(w[:, s, :, :], a["L3_gnn_weight"][:, s * P:(s + 1) * P, :]
                                 .rearrange("r p o -> p r o")).then_inc(loaded, 16)
            else:
                sp.dma_start(w[:, 0, :, :], a["L1_gnn_basis"].rearrange("b i o -> (b i) o")
                             .rearrange("(r p) o -> p r o", p=P)).then_inc(loaded, 16)
                for n in range(P // R):
                    sp.dma_start(comp[n * R:(n + 1) * R, :], a["L1_gnn_w_comp"]).then_inc(loaded, 16)
            def store(t, q):
                sp.wait_ge(low_out, t + 2)
                sp.wait_ge(high_out, t + 2)
                sp.dma_start(t_dram.ap()[bass.ds(t * (P * R), P * R), :].rearrange("(p r) d -> p (r d)", r=R),
                             table[:, q, :, :].rearrange("p r d -> p (r d)")).then_inc(stored[q], 16)

            with sp.Fori(0, T // 2) as t:
                for q in range(2):
                    store(t * 2 + q, q)
            store(T - 1, 0)
            sp.wait_ge(stored[0], 16 * (T // 2 + 1))
            sp.wait_ge(stored[1], 16 * (T // 2))

        @block.gpsimd
        def _(pool):
            if not relational:
                pool.wait_ge(loaded, loads)
                for s in range(2):
                    nc.gpsimd.tensor_copy(mix[:, s, :].rearrange("p (j b) -> p j b", b=NB),
                                          comp[:].unsqueeze(1).broadcast_to([P, P // NB, NB])).then_inc(made, 1)
                pool.wait_ge(made, 2)
                for s in range(2):
                    v = mix[:, s, :].rearrange("p (j b) -> p j b", b=NB)
                    nc.gpsimd.affine_select(out=v, in_=v, compare_op=ALU.is_ge, fill=0.0, base=P * s,
                                            pattern=[[-R, P // NB], [0, NB]], channel_multiplier=1).then_inc(made, 1)
                pool.wait_ge(made, 4)
                for s in range(2):
                    v = mix[:, s, :].rearrange("p (j b) -> p j b", b=NB)
                    nc.gpsimd.affine_select(out=v, in_=v, compare_op=ALU.is_ge, fill=0.0, base=R - 1 - P * s,
                                            pattern=[[R, P // NB], [0, NB]], channel_multiplier=-1).then_inc(made, 1)

        @block.tensor
        def _(pe):
            pe.wait_ge(loaded, loads)
            if not relational:
                pe.wait_ge(made, 6)
            with pe.Fori(0, T) as t:
                pe.wait_ge(staged, t + 1)
                for s in range(2):
                    last = nc.tensor.transpose(p_t[:, s, :], tile[:, s * P:(s + 1) * P], g.ident[:])
                last.then_inc(turn, 1)
                pe.wait_ge(back, t + 1)
                if not relational:
                    for s in range(2):
                        last = nc.tensor.matmul(p_m[:], mix[:, s, :], turned[:, s, :], start=s == 0, stop=s == 1)
                    last.then_inc(mixing, 1)
                    pe.wait_ge(unmixed, t + 1)
                pe.wait_ge(low_out, t + 1)
                pe.wait_ge(high_out, t + 1)
                for q in range(4):
                    for s in range(parts):
                        last = nc.tensor.matmul(p_o[:, q, :, :], turned[:, s, :] if relational else mixed[:],
                                                w[:, s, 2 * q:2 * q + 2, :], start=s == 0, stop=s == parts - 1)
                    if q % 2:
                        last.then_inc(product, 1)

        @block.scalar
        def _(act):
            act.sem_inc(low_out, 1)

            def tile_work(t, q, refill):
                act.wait_ge(turn, t + 1)
                nc.scalar.copy(turned[:], p_t[:]).then_inc(back, 1)
                act.wait_ge(product, t * 2 + 1)
                if refill is not None:
                    act.wait_ge(stored[q], refill)
                nc.scalar.copy(table[:, q, 0:4, :], p_o[:, 0:2, :, :].rearrange("p a b d -> p (a b) d")
                               ).then_inc(low_out, 1)

            for q in range(2):
                tile_work(q, q, None)
            with act.Fori(1, T // 2) as i:
                for q in range(2):
                    tile_work(i * 2 + q, q, i * 16)
            tile_work(T - 1, 0, 16 * (T // 2))

        @block.vector
        def _(dve):
            dve.sem_inc(high_out, 1)
            nc.vector.memset(g.acc[:], 0.0)
            nc.vector.tensor_copy(tile[:], g.x[:, 0, :]).then_inc(staged, 1)

            def tile_work(t, q, refill, more):
                if not relational:
                    dve.wait_ge(mixing, t + 1)
                    nc.vector.tensor_copy(mixed[:], p_m[:]).then_inc(unmixed, 1)
                if more:
                    dve.wait_ge(turn, t + 1)
                    nc.vector.tensor_copy(tile[:], g.x[:, bass.ds(t + 1, 1), :].rearrange("p t d -> p (t d)")
                                          ).then_inc(staged, 1)
                dve.wait_ge(product, t * 2 + 2)
                if refill is not None:
                    dve.wait_ge(stored[q], refill)
                nc.vector.tensor_copy(table[:, q, 4:8, :], p_o[:, 2:4, :, :].rearrange("p a b d -> p (a b) d")
                                      ).then_inc(high_out, 1)

            for q in range(2):
                tile_work(q, q, None, True)
            with dve.Fori(1, T // 2) as i:
                for q in range(2):
                    tile_work(i * 2 + q, q, i * 16, True)
            tile_work(T - 1, 0, 16 * (T // 2), False)


def relu_update(nc, g, tag, bias_ap, after=None, out=None):
    with ExitStack() as ctx:
        m = Mem(nc, ctx, tag)
        bias = m.sb("bias", [P, D])
        loaded, vec, ready, stored = m.sem("loaded"), m.sem("vec"), m.sem("ready"), m.sem("stored")
        roots, ln = Roots(nc, m), NormTiles(m)
        block = ctx.enter_context(nc.Block())

        @block.scalar
        def _(act):
            roots.root(act, ln.root[:], ln.var[:])

        @block.sync
        def _(sp):
            sp.dma_start(bias[:], row_of_all(bias_ap)).then_inc(loaded, 16)
            if out is not None:
                sp.wait_ge(ready, 1)
                sp.dma_start(out[0:(T - 1) * P, :].rearrange("(t p) d -> p t d", p=P), g.x[:, 0:T - 1, :]
                             ).then_inc(stored, 16)
                sp.dma_start(out[(T - 1) * P:N, :], g.x[0:LAST, T - 1, :]).then_inc(stored, 16)
                sp.wait_ge(stored, 32)

        @block.vector
        def _(dve):
            c = Count(dve, vec)
            v = Vector(nc, dve, c, roots)
            dve.wait_ge(loaded, 16)
            acc = g.acc[:, 0:T, 0:D]
            v.tt(acc, acc, over_tiles(bias[:]), ALU.add)
            v.ts(acc, acc, 0.0, ALU.max)
            v.tt(g.x[:], g.x[:], acc, ALU.add)
            normalise(nc, g, ln, dve, c, v)
            dve.sem_inc(ready, 1)


def hyperbolic_prepare(nc, g, a, lx_dram, msg_dram, sj_dram):
    with ExitStack() as ctx:
        m = Mem(nc, ctx, "hyp")
        w = m.sb("w", [P, 2, D])
        hb = m.sb("hb", [P, D])
        att = m.sb("att", [P, H, 2 * DH])
        tile = m.sb("tile", [P, D])
        turned = m.sb("turned", [P, 2, P])
        p_t = m.ps("p_t", [P, 4, P])
        p_w = m.ps("p_w", [P, 512])
        loaded, staged, turn, back, product, copied, vec, logs, lx_out, lx_in, scored, tables, thrown, tanhs, lns = (
            m.sem(n) for n in ("loaded", "staged", "turn", "back", "product", "copied", "vec", "logs", "lx_out",
                               "lx_in", "scored", "tables", "thrown", "tanhs", "lns"))
        logs_of = {n: m.sem(f"log_of_{n}") for n in "xur"}
        names = ("xx", "nw", "rr", "ww", "wb", "nx", "fx", "nu", "c", "t1", "t2", "t3", "A", "B", "nr")
        s = {n: m.sb(n, [P, T]) for n in names}
        b = {n: m.sb("b_" + n, [P, 1]) for n in ("bb", "nb", "c", "t1")}
        roots = Roots(nc, m)
        y, tmp = g.y, g.tmp
        block = ctx.enter_context(nc.Block())
        flat = lx_dram.ap().rearrange("n (q d) -> (n q) d", d=DH)

        @block.sync
        def _(sp):
            sp.dma_start(w[:], a["L2_gnn_W_T"].rearrange("(s p) o -> p s o", p=P)).then_inc(loaded, 16)
            sp.dma_start(hb[:], row_of_all(a["L2_gnn_b_lin"])).then_inc(loaded, 16)
            sp.dma_start(att[:].rearrange("p h d -> p (h d)"),
                         row_of_all(a["L2_gnn_att"].rearrange("h d -> (h d)"))).then_inc(loaded, 16)
            sp.wait_ge(logs, 1)
            sp.dma_start(lx_dram.ap().rearrange("(t p) d -> p t d", p=P), y).then_inc(lx_out, 16)
            sp.wait_ge(lx_out, 16)
            for h in range(H):
                sp.dma_start(y[:, 0:T - 1, h * DH:(h + 1) * DH],
                             flat[h * N:h * N + (T - 1) * P, :].rearrange("(t p) d -> p t d", p=P)).then_inc(lx_in, 16)
                sp.dma_start(y[0:LAST, T - 1, h * DH:(h + 1) * DH],
                             flat[h * N + (T - 1) * P:(h + 1) * N, :]).then_inc(lx_in, 16)
            sp.wait_ge(scored, 1)
            sp.wait_ge(lx_in, 128)
            sp.dma_start(msg_dram.ap()[:, 0:D].rearrange("(t p) d -> p t d", p=P), y).then_inc(tables, 16)
            sp.dma_start(msg_dram.ap()[:, D:D + H].rearrange("(t p) d -> p t d", p=P), g.sj[:]).then_inc(tables, 16)
            sp.dma_start(sj_dram.ap().rearrange("(t p) d -> p t d", p=P), g.sj[:]).then_inc(tables, 16)
            sp.wait_ge(tables, 48)

        @block.tensor
        def _(pe):
            pe.wait_ge(loaded, 48)
            with pe.Fori(0, T) as t:
                pe.wait_ge(staged, t + 1)
                for q in range(2):
                    last = nc.tensor.transpose(p_t[:, q, :], tile[:, q * P:(q + 1) * P], g.ident[:])
                last.then_inc(turn, 1)
                pe.wait_ge(back, t + 1)
                pe.wait_ge(copied, t + 1)
                for q in range(2):
                    last = nc.tensor.matmul(p_w[:, 0:D], turned[:, q, :], w[:, q, :], start=q == 0, stop=q == 1)
                last.then_inc(product, 1)

        @block.scalar
        def _(act):
            act.sem_inc(copied, 1)
            with act.Fori(0, T) as t:
                act.wait_ge(turn, t + 1)
                nc.scalar.copy(turned[:], p_t[:, 0:2, :]).then_inc(back, 1)
                act.wait_ge(product, t + 1)
                nc.scalar.copy(y[:, bass.ds(t, 1), :].rearrange("p t d -> p (t d)"), p_w[:, 0:D]).then_inc(copied, 1)
            roots.root(act, b["nb"][:], b["bb"][:])
            roots.root(act, s["nx"][:], s["xx"][:])
            act.wait_ge(logs_of["x"], 1)
            nc.scalar.activation(s["t1"][:], s["t1"][:], ACT.Ln).then_inc(lns, 1)
            roots.root(act, s["nw"][:], s["ww"][:])
            act.wait_ge(logs_of["u"], 1)
            nc.scalar.activation(s["t1"][:], s["nu"][:], ACT.Tanh).then_inc(tanhs, 1)
            nc.scalar.activation(b["t1"][:], b["nb"][:], ACT.Tanh).then_inc(tanhs, 1)
            roots.root(act, b["nb"][:], b["bb"][:])
            roots.root(act, s["nr"][:], s["rr"][:])
            act.wait_ge(logs_of["r"], 1)
            nc.scalar.activation(s["t1"][:], s["t1"][:], ACT.Ln).then_inc(lns, 1)

        @block.vector
        def _(dve):
            c = Count(dve, vec)
            v = Vector(nc, dve, c, roots)
            nc.vector.tensor_copy(tile[:], g.x[:, 0, :]).then_inc(staged, 1)
            with dve.Fori(1, T) as t:
                dve.wait_ge(turn, t)
                nc.vector.tensor_copy(tile[:], g.x[:, bass.ds(t, 1), :].rearrange("p t d -> p (t d)")
                                      ).then_inc(staged, 1)

            def clipped_root(out, x, t):
                v.sqrt(out, x, t)
                v.ts(out, out, 1e-15, ALU.max)

            def arctanh_over(out, n, which, t1, t2, t3, turn_no):
                y1 = out
                v.ts(y1, n, LARGEST, ALU.min)
                v.ts(t1, y1, -1.0, ALU.mult, 1.0, ALU.add)
                v.recip(t1, t1)
                v.ts(t2, y1, 1.0, ALU.add)
                v.tt(t1, t1, t2, ALU.mult)
                dve.sem_inc(logs_of[which], 1)
                v.tt(t2, y1, y1, ALU.mult)
                v.ts(t3, t2, 1.0 / 15, ALU.mult, 1.0 / 13, ALU.add)
                for k in (11, 9, 7, 5, 3, 1):
                    v.tt(t3, t3, t2, ALU.mult)
                    v.ts(t3, t3, 1.0 / k, ALU.add)
                v.recip(t2, n)
                v.tt(t3, t3, y1, ALU.mult)
                dve.wait_ge(lns, turn_no)
                v.ts(t1, t1, 0.5, ALU.mult)
                v.tt(t1, t1, t3, ALU.subtract)
                v.ts(y1, y1, 0.3, ALU.is_ge)
                v.tt(t1, t1, y1, ALU.mult)
                v.tt(t1, t1, t3, ALU.add)
                v.tt(out, t1, t2, ALU.mult)

            S = {n: t[:] for n, t in s.items()}
            B1 = {n: t[:] for n, t in b.items()}
            dve.wait_ge(loaded, 48)
            v.tt(tmp, g.x[:], g.x[:], ALU.mult)
            v.row_sum(S["xx"], tmp)
            v.tt(tmp[:, 0, :], hb[:], hb[:], ALU.mult)
            v.row_sum(B1["bb"], tmp[:, 0, :])
            clipped_root(B1["nb"], B1["bb"], B1["t1"])
            clipped_root(S["nx"], S["xx"], S["t1"])
            arctanh_over(S["fx"], S["nx"], "x", S["t1"], S["t2"], S["t3"], 1)
            dve.wait_ge(copied, T + 1)
            v.tt(tmp, y, y, ALU.mult)
            v.row_sum(S["ww"], tmp)
            v.sqrt(S["nw"], S["ww"], S["t1"])
            v.tt(S["nu"], S["nw"], S["fx"], ALU.mult)
            v.ts(S["nu"], S["nu"], 1e-15, ALU.max)
            dve.sem_inc(logs_of["u"], 1)
            v.recip(S["t2"], S["nu"])
            v.tt(S["t2"], S["t2"], S["fx"], ALU.mult)
            dve.wait_ge(tanhs, 2)
            v.tt(S["c"], S["t1"], S["t2"], ALU.mult)
            v.tt(S["t1"], S["c"], S["nw"], ALU.mult)
            v.ts(S["t1"], S["t1"], 1e-15, ALU.max)
            v.to_one(S["c"], S["t1"], MAXN, S["t2"])
            v.recip(B1["c"], B1["nb"])
            v.tt(B1["c"], B1["c"], B1["t1"], ALU.mult)
            v.ts(hb[:], hb[:], B1["c"], ALU.mult)
            v.tt(tmp[:, 0, :], hb[:], hb[:], ALU.mult)
            v.row_sum(B1["bb"], tmp[:, 0, :])
            clipped_root(B1["nb"], B1["bb"], B1["t1"])
            v.ts(B1["c"], B1["c"], 0.0, ALU.mult, 1.0, ALU.add)
            v.to_one(B1["c"], B1["nb"], MAXN, B1["t1"])
            v.ts(hb[:], hb[:], B1["c"], ALU.mult)
            v.tt(tmp[:, 0, :], hb[:], hb[:], ALU.mult)
            v.row_sum(B1["bb"], tmp[:, 0, :])
            v.tt(tmp, y, over_tiles(hb[:]), ALU.mult)
            v.row_sum(S["wb"], tmp)
            v.tt(S["t1"], S["c"], S["nw"], ALU.mult)
            v.tt(S["t1"], S["t1"], S["t1"], ALU.mult)
            v.tt(S["t2"], S["c"], S["wb"], ALU.mult)
            v.ts(S["t2"], S["t2"], 2.0, ALU.mult, 1.0, ALU.add)
            v.stt(S["t3"], S["t1"], B1["bb"], S["t2"], ALU.mult, ALU.add)
            v.ts(S["t3"], S["t3"], 1e-15, ALU.max)
            v.recip(S["t3"], S["t3"])
            v.stt(S["A"], S["t2"], B1["bb"], S["t3"], ALU.add, ALU.mult)
            v.tt(S["A"], S["A"], S["c"], ALU.mult)
            v.ts(S["t1"], S["t1"], -1.0, ALU.mult, 1.0, ALU.add)
            v.tt(S["B"], S["t1"], S["t3"], ALU.mult)
            v.tt(y, y, over_features(S["A"]), ALU.mult)
            v.tt(tmp, over_tiles(hb[:]), over_features(S["B"]), ALU.mult)
            v.tt(y, y, tmp, ALU.add)
            v.tt(tmp, y, y, ALU.mult)
            v.row_sum(S["rr"], tmp)
            clipped_root(S["nr"], S["rr"], S["t1"])
            v.ts(S["c"], S["nr"], 0.0, ALU.mult, 1.0, ALU.add)
            v.to_one(S["c"], S["nr"], MAXN, S["t1"])
            v.tt(S["nr"], S["nr"], S["c"], ALU.mult)
            v.ts(S["nr"], S["nr"], 1e-15, ALU.max)
            arctanh_over(S["fx"], S["nr"], "r", S["t1"], S["t2"], S["t3"], 2)
            v.tt(S["c"], S["c"], S["fx"], ALU.mult)
            v.tt(y, y, over_features(S["c"]), ALU.mult)
            dve.sem_inc(logs, 1)
            dve.wait_ge(lx_in, 128)
            y4 = y.rearrange("p t (h d) -> p t h d", h=H)
            tmp4 = tmp.rearrange("p t (h d) -> p t h d", h=H)
            for lo, out in ((0, g.si), (DH, g.sj)):
                for h in range(H):
                    v.tt(tmp4[:, :, h, :], y4[:, :, h, :], over_tiles(att[:, h, lo:lo + DH]), ALU.mult)
                v.row_sum(out[:].rearrange("p t h -> p (t h)"), tmp.rearrange("p t (h d) -> p (t h) d", h=H))
            dve.sem_inc(scored, 1)


def neighbour_max(nc, g, sj_dram):
    PER = GRP * H
    with ExitStack() as ctx:
        m = Mem(nc, ctx, "nmax")
        rows = m.sb("rows", [P, BODY, H])
        ring_row = m.sb("ring_row", [P, BODY], I32)
        away = m.sb("away", [P, BODY, P])
        minus_local = m.sb("minus_local", [P, CHP])
        four = m.sb("four", [P, H, P])
        best = m.sb("best", [P, T, H])
        tmp = m.sb("tmp", [P, T, H])
        rest = m.sb("rest", [P, (T + 1) * 2 * H])
        p_t = m.ps("p_t", [P, 2, H, P])
        staged, tick, taken, vec, copied, turn, reduced, placed, away_ready = (m.sem(n) for n in (
            "staged", "tick", "taken", "vec", "copied", "turn", "reduced", "placed", "away_ready"))
        landed = [m.sem(f"landed_{r}") for r in range(RING)]
        block = ctx.enter_context(nc.Block())
        low = g.big[:, 0:(T + 1) * H * P].rearrange("p (t h n) -> p t h n", h=H, n=P)

        @block.scalar
        def _(act):
            def stage(at, r):
                nc.scalar.copy(ring_row[:, r * GRP:(r + 1) * GRP],
                               g.rec[0][:, bass.ds(at, GRP), 0]).then_inc(staged, 1)

            act.wait_ge(placed, 1)

            def distance(at, r):
                for q in range(GRP):
                    last = nc.scalar.activation(away[:, r * GRP + q, :], g.iota[:, 0:P], ACT.Abs, scale=STEP,
                                                bias=minus_local[:, bass.ds(at + q, 1)])
                last.then_inc(away_ready, 1)

            for r in range(RING):
                stage(r * GRP, r)
                distance(r * GRP, r)
            with act.Fori(1, LOOPS) as i:
                for r in range(RING):
                    act.wait_ge(taken, i * (RING * PER) + (r + 1 - RING) * PER)
                    stage(i * BODY + r * GRP, r)
                    distance(i * BODY + r * GRP, r)
            act.wait_ge(taken, LOOPS * RING * PER)
            act.sem_inc(turn, 1)
            with act.Fori(0, T) as t:
                act.wait_ge(turn, t + 1)
                nc.scalar.copy(four[:].rearrange("p h n -> p (h n)"),
                               low[:, bass.ds(t, 1), :, :].rearrange("p t h n -> p (t h n)")).then_inc(copied, 1)

        @block.gpsimd
        def _(pool):
            with pool.Fori(0, LOOPS) as i:
                for r in range(RING):
                    pool.wait_ge(staged, i * RING + (r + 1))
                    pool.sem_inc(tick, 1)
                    for j in range(r * GRP, (r + 1) * GRP):
                        pool.indirect_dma_start(rows[:, j, :], None, sj_dram.ap(), bass.IndirectOffsetOnAxis(
                            ap=ring_row[:, j:j + 1], axis=0)).then_inc(landed[r], 16)

        @block.tensor
        def _(pe):
            with pe.Fori(0, T) as t:
                pe.wait_ge(copied, t + 1)
                pe.wait_ge(reduced, t + 1)
                for h in range(H):
                    last = nc.tensor.transpose(p_t[:, 0, h, :], four[:, h, :], g.ident[:])
                last.then_inc(turn, 1)

        @block.vector
        def _(dve):
            c = Count(dve, vec)
            v = Vector(nc, dve, c)
            nc.vector.tensor_scalar(minus_local[:], g.rec[0][:, :, 2], -STEP, None, ALU.mult).then_inc(placed, 1)
            v.did(nc.vector.memset(g.big[:, 0:(T + 1) * H * P], STEP))
            t = Count(dve, taken)

            def turn_of(i):
                t.enter(i, RING * PER)
                tiles = tiles_of(nc, mybir.EngineType.DVE, g.pair_tile[0], i * (BODY // 2), BODY // 2)
                for r in range(RING):
                    dve.wait_ge(away_ready, i * RING + (r + 1))
                    dve.wait_ge(landed[r], i * (16 * GRP) + 16 * GRP)
                    for q in range(GRP):
                        for h in range(H):
                            if not (isinstance(i, int) and i + r + q == 0):
                                t.wait(H - 1)
                            at = low[:, bass.ds(tiles[2 * r + q // 2], 1), h, :].rearrange("p t n -> p (t n)")
                            t.step(nc.vector.scalar_tensor_tensor(at, away[:, r * GRP + q, :],
                                                                  rows[:, r * GRP + q, h:h + 1], at,
                                                                  ALU.subtract, ALU.min))

            turn_of(0)
            with dve.Fori(1, LOOPS) as i:
                turn_of(i)
            t.leave(LOOPS)
            t.wait()
            dve.sem_inc(reduced, 1)
            with dve.Fori(0, T) as t:
                dve.wait_ge(turn, t + 2)
                nc.vector.tensor_reduce(best[:, bass.ds(t, 1), :].rearrange("p t h -> p (t h)"), p_t[:, 0, :, :],
                                        AX.X, ALU.min).then_inc(reduced, 1)
            dve.wait_ge(reduced, T + 1)
            si, top = g.sm[:, 0:T, 0:H], g.sm[:, 0:T, H:2 * H]
            v.did(nc.vector.memset(g.sm[:], 0.0))
            v.did(nc.vector.tensor_copy(si, g.si[:]))
            v.stt(best[:], best[:], -1.0, g.sj[:], ALU.mult, ALU.max)
            v.tt(best[:], best[:], g.si[:], ALU.add)
            v.ts(tmp[:], best[:], 0.2, ALU.mult)
            v.tt(top, best[:], tmp[:], ALU.max)
            sm = g.sm[:].rearrange("p t s -> p (t s)")
            sm3 = g.sm3[:].rearrange("p t (s n) -> p (t s) n", n=3)
            v.did(nc.vector.tensor_copy(rest[:], sm))
            for n in range(3):
                v.did(nc.vector.tensor_copy(sm3[:, :, n], rest[:]))
                if n < 2:
                    v.tt(rest[:], rest[:], sm3[:, :, n], ALU.subtract)


def attend(nc, g, msg_dram):
    W = D + H
    PARTS = 3 * 2 * H
    with ExitStack() as ctx:
        m = Mem(nc, ctx, "att")
        rows = m.sb("rows", [P, BODY, W])
        weighted = m.sb("weighted", [P, BODY, W])
        hot_b = m.sb("hot_b", [P, BODY, P], BF16)
        hot = m.sb("hot", [P, BODY, P])
        hot_t = m.sb("hot_t", [P, 2, GRP, P], BF16)
        seen = m.sb("seen", [P, GRP, 2 * H])
        alpha = m.sb("alpha", [P, 2, GRP, H])
        slope = m.sb("slope", [P, GRP, H])
        ring_row = m.sb("ring_row", [P, BODY], I32)
        sums = m.ps("sums", [P, 4, 512])
        p_t = m.ps("p_t", [P, 2, 2 * GRP, P], BF16)
        p_s = m.ps("p_s", [P, 2, 512])
        (staged, tick, hot_ready, widened, turn, back, looked, alphas, exps, ready, summed, added, vec, psum_free) = (
            m.sem(n) for n in ("staged", "tick", "hot_ready", "widened", "turn", "back", "looked", "alphas", "exps", "ready",
                               "summed", "added", "vec", "psum_free"))
        landed = [m.sem(f"landed_{r}") for r in range(RING)]
        block = ctx.enter_context(nc.Block())

        @block.gpsimd
        def _(pool):
            with pool.Fori(0, LOOPS) as i:
                for r in range(RING):
                    pool.wait_ge(staged, i * RING + (r + 1))
                    pool.sem_inc(tick, 1)
                    for j in range(r * GRP, (r + 1) * GRP):
                        pool.indirect_dma_start(rows[:, j, :], None, msg_dram.ap(), bass.IndirectOffsetOnAxis(
                            ap=ring_row[:, j:j + 1], axis=0)).then_inc(landed[r], 16)

        @block.scalar
        def _(act):
            def stage(at, r):
                nc.scalar.copy(ring_row[:, r * GRP:(r + 1) * GRP],
                               g.rec[0][:, bass.ds(at, GRP), 0]).then_inc(staged, 1)

            for r in range(RING):
                stage(r * GRP, r)

            def back_of(i, r):
                act.wait_ge(turn, i * RING + (r + 1))
                nc.scalar.copy(hot_t[:, r % 2, :, :], p_t[:, r % 2, 0:GRP, :]).then_inc(back, 1)

            def widen(i, r):
                act.wait_ge(hot_ready, i * RING + (r + 1))
                s = slice((r % RING) * GRP, (r % RING + 1) * GRP)
                nc.scalar.copy(hot[:, s, :], hot_b[:, s, :]).then_inc(widened, 1)

            def turn_of(i, first=False, last=False):
                for r in range(RING):
                    if not (last and r == RING - 1):
                        back_of(i, r + 1)
                        widen(i, r + 1)
                    act.wait_ge(alphas, i * RING + (r + 1))
                    nc.scalar.activation(weighted[:, r * GRP:(r + 1) * GRP, D:W], alpha[:, r % 2, :, :],
                                         ACT.Exp).then_inc(exps, 1)
                    if not (first and r == 0 or last and r > 0):
                        act.wait_ge(ready, i * RING + r)
                        stage(i * BODY + ((r - 1) * GRP + BODY), (r - 1) % RING)

            back_of(0, 0)
            widen(0, 0)
            turn_of(0, first=True)
            with act.Fori(1, LOOPS - 1) as i:
                turn_of(i)
            turn_of(LOOPS - 1, last=True)

        @block.tensor
        def _(pe):
            def turn_over(i, r):
                pe.wait_ge(hot_ready, i * RING + (r + 1))
                for q in range(GRP):
                    last = nc.tensor.transpose(p_t[:, r % 2, q, :], hot_b[:, (r % RING) * GRP + q, :], g.ident_b[:])
                last.then_inc(turn, 1)

            def look(i, r, tiles):
                pe.wait_ge(back, i * RING + (r + 1))
                for q in range(GRP):
                    last = nc.tensor.matmul(p_s[:, r % 2, PARTS * q:PARTS * (q + 1)], hot_t[:, r % 2, q, :],
                                            g.sm3[:, bass.ds(tiles[q // 2], 1), :].rearrange("p t s -> p (t s)"),
                                            start=True, stop=True)
                last.then_inc(looked, 1)

            def turn_of(i, last_turn=False):
                tiles = tiles_of(nc, mybir.EngineType.PE, g.pair_tile[0], i * (BODY // 2) + 2, BODY // 2)
                for r in range(RING):
                    n = i * RING + (r + 1)
                    if not (last_turn and r >= RING - 2):
                        turn_over(i, r + 2)
                    if not (last_turn and r == RING - 1):
                        look(i, r + 1, tiles[2 * r:2 * r + 2])
                    pe.wait_ge(widened, n)
                    pe.wait_ge(ready, n)
                    pe.wait_ge(psum_free, n)
                    for q in range(GRP):
                        last = nc.tensor.matmul(sums[:, 2 * (r % 2) + q // 2, 0:W], hot[:, r * GRP + q, :],
                                                weighted[:, r * GRP + q, :], start=q % 2 == 0, stop=q % 2 == 1)
                    last.then_inc(summed, 1)

            turn_over(0, 0)
            look(0, 0, tiles_of(nc, mybir.EngineType.PE, g.pair_tile[0], 0, 2))
            turn_over(0, 1)
            with pe.Fori(0, LOOPS - 1) as i:
                turn_of(i)
            turn_of(LOOPS - 1, True)

        @block.vector
        def _(dve):
            c = Count(dve, vec)
            v = Vector(nc, dve, c)

            def one_hot(i, r, q):
                made = nc.vector.tensor_scalar(hot_b[:, (r % RING) * GRP + q, :], g.iota_b[:],
                                               g.rec[0][:, bass.ds(i * BODY + (r * GRP + q), 1), 2], None,
                                               ALU.is_equal)
                if q == GRP - 1:
                    made.then_inc(hot_ready, 1)

            def build(i, r):
                for q in range(GRP):
                    one_hot(i, r, q)

            def add(i, r, tiles):
                dve.wait_ge(summed, i * RING + (r + 1))
                for q in range(2):
                    if not (isinstance(i, int) and i + r + q == 0):
                        dve.wait_ge(added, i * (2 * RING) + (2 * r + q))
                    at = g.acc[:, bass.ds(tiles[q], 1), 0:W].rearrange("p t d -> p (t d)")
                    nc.vector.tensor_tensor(at, sums[:, 2 * (r % 2) + q, 0:W], at, ALU.add).then_inc(added, 1)
                dve.wait_ge(added, i * (2 * RING) + (2 * r + 2))
                dve.sem_inc(psum_free, 1)

            def scores(i, r, one_hot=None):
                n, al = i * RING + (r + 1), alpha[:, r % 2, :, :]
                at = r % RING * GRP
                dve.wait_ge(landed[r % RING], (i + r // RING) * (16 * GRP) + 16 * GRP)
                dve.wait_ge(looked, n)

                def then(ins, q=None):
                    c.step(ins)
                    if one_hot and q is not None:
                        one_hot(q)
                    c.wait()

                then(nc.vector.tensor_reduce(
                    seen[:].rearrange("p q s -> p (q s)"),
                    p_s[:, r % 2, 0:PARTS * GRP].rearrange("p (s n) -> p s n", n=3), AX.X, ALU.add), 0)
                then(nc.vector.tensor_tensor(al, rows[:, at:at + GRP, D:W], seen[:, :, 0:H], ALU.add), 1)
                then(nc.vector.tensor_scalar(slope[:], al, 0.2, None, ALU.mult), 2)
                then(nc.vector.tensor_tensor(al, al, slope[:], ALU.max), 3)
                then(nc.vector.tensor_tensor(al, al, seen[:, :, H:2 * H], ALU.subtract))
                dve.sem_inc(alphas, 1)

            def turn_of(i, first=False, last_turn=False):
                if not last_turn:
                    c.enter(i, RING * 5)
                if first:
                    tiles = (None, None, *tiles_of(nc, mybir.EngineType.DVE, g.pair_tile[0], 0, BODY // 2 - 2))
                else:
                    tiles = tiles_of(nc, mybir.EngineType.DVE, g.pair_tile[0], i * (BODY // 2) - 2, BODY // 2)
                for r in range(RING):
                    dve.wait_ge(exps, i * RING + (r + 1))
                    for q in range(r * GRP, (r + 1) * GRP):
                        last = nc.vector.tensor_tensor(
                            weighted[:, q, 0:D].rearrange("p (h d) -> p h d", h=H),
                            rows[:, q, 0:D].rearrange("p (h d) -> p h d", h=H),
                            weighted[:, q, D:W].unsqueeze(2).broadcast_to([P, H, DH]), ALU.mult)
                    last.then_inc(ready, 1)
                    if not (last_turn and r == RING - 1):
                        more = not (last_turn and r >= RING - 3)
                        scores(i, r + 1, (lambda q: one_hot(i, r + 3, q)) if more else None)
                    if not (first and r == 0):
                        before = tiles[2 * r:2 * r + 2]
                        add(i, r - 1, before) if r else add(i - 1, RING - 1, before)

            dve.sem_inc(psum_free, 2)
            build(0, 0)
            build(0, 1)
            build(0, 2)
            scores(0, 0)
            turn_of(0, first=True)
            with dve.Fori(1, LOOPS - 1) as i:
                turn_of(i)
            c.leave(LOOPS - 1)
            turn_of(LOOPS - 1, last_turn=True)
            add(LOOPS - 1, RING - 1, tiles_of(nc, mybir.EngineType.DVE, g.pair_tile[0],
                                              LOOPS * (BODY // 2) - 2, 2))


def hyperbolic_finish(nc, g, a, msg_dram, o_dram):
    W = D + H
    with ExitStack() as ctx:
        m = Mem(nc, ctx, "fin")
        bias = m.sb("bias", [P, D])
        own = m.sb("own", [P, T, H])
        tmp_h = m.sb("tmp_h", [P, T, H])
        total = m.sb("total", [P, T, H])
        square, norm, scale, t1 = (m.sb(n, [P, T]) for n in ("square", "norm", "scale", "t1"))
        roots, ln = Roots(nc, m), NormTiles(m)
        loaded, alphas, exps, vec, divided, out_stored, out_in, norms, tanhs = (m.sem(n) for n in (
            "loaded", "alphas", "exps", "vec", "divided", "out_stored", "out_in", "norms", "tanhs"))
        block = ctx.enter_context(nc.Block())
        y, tmp = g.y, g.tmp
        flat = o_dram.ap().rearrange("n (q d) -> (n q) d", d=DH)

        @block.sync
        def _(sp):
            sp.dma_start(bias[:], row_of_all(a["L2_gnn_b_conv"])).then_inc(loaded, 16)
            sp.dma_start(y, msg_dram.ap()[:, 0:D].rearrange("(t p) d -> p t d", p=P)).then_inc(loaded, 16)
            sp.wait_ge(divided, 1)
            for h in range(H):
                sp.dma_start(flat[h * N:h * N + (T - 1) * P, :].rearrange("(t p) d -> p t d", p=P),
                             y[:, 0:T - 1, h * DH:(h + 1) * DH]).then_inc(out_stored, 16)
                sp.dma_start(flat[h * N + (T - 1) * P:(h + 1) * N, :],
                             y[0:LAST, T - 1, h * DH:(h + 1) * DH]).then_inc(out_stored, 16)
            sp.wait_ge(out_stored, 128)
            sp.dma_start(y[:, 0:T - 1, :], o_dram.ap()[0:(T - 1) * P, :].rearrange("(t p) d -> p t d", p=P)
                         ).then_inc(out_in, 16)
            sp.dma_start(y[0:LAST, T - 1, :], o_dram.ap()[(T - 1) * P:N, :]).then_inc(out_in, 16)

        @block.scalar
        def _(act):
            act.wait_ge(alphas, 1)
            nc.scalar.activation(own[:], own[:], ACT.Exp).then_inc(exps, 1)
            roots.root(act, norm[:], square[:])
            act.wait_ge(norms, 1)
            nc.scalar.activation(t1[:], norm[:], ACT.Tanh).then_inc(tanhs, 1)
            roots.root(act, ln.root[:], ln.var[:])

        @block.vector
        def _(dve):
            c = Count(dve, vec)
            v = Vector(nc, dve, c, roots)
            v.tt(own[:], g.si[:], g.sj[:], ALU.add)
            v.ts(tmp_h[:], own[:], 0.2, ALU.mult)
            v.tt(own[:], own[:], tmp_h[:], ALU.max)
            v.tt(own[:], own[:], g.sm[:, 0:T, H:2 * H], ALU.subtract)
            dve.sem_inc(alphas, 1)
            dve.wait_ge(exps, 1)
            dve.wait_ge(loaded, 32)
            v.tt(total[:], g.acc[:, 0:T, D:W], own[:], ALU.add)
            v.ts(total[:], total[:], 1e-15, ALU.max)
            v.recip(total[:], total[:])
            for h in range(H):
                cols = slice(h * DH, (h + 1) * DH)
                v.tt(y[:, :, cols], y[:, :, cols], over_features(own[:, :, h], DH), ALU.mult)
                v.tt(y[:, :, cols], y[:, :, cols], g.acc[:, 0:T, cols], ALU.add)
                v.tt(y[:, :, cols], y[:, :, cols], over_features(total[:, :, h], DH), ALU.mult)
            dve.sem_inc(divided, 1)
            dve.wait_ge(out_in, 32)
            v.tt(y, y, over_tiles(bias[:]), ALU.add)
            v.ts(y, y, 0.0, ALU.max)
            v.tt(tmp, y, y, ALU.mult)
            v.row_sum(square[:], tmp)
            v.sqrt(norm[:], square[:], t1[:])
            v.ts(norm[:], norm[:], 1e-15, ALU.max)
            dve.sem_inc(norms, 1)
            v.recip(scale[:], norm[:])
            dve.wait_ge(tanhs, 1)
            v.tt(scale[:], scale[:], t1[:], ALU.mult)
            v.tt(norm[:], norm[:], scale[:], ALU.mult)
            v.ts(norm[:], norm[:], 1e-15, ALU.max)
            v.to_one(scale[:], norm[:], MAXN, t1[:])
            v.tt(y, y, over_features(scale[:]), ALU.mult)
            v.tt(g.x[:], g.x[:], y, ALU.add)
            normalise(nc, g, ln, dve, c, v)


def build(nc, a, out):
    dram = lambda name, shape: nc.dram_tensor(name, shape, F32)
    h_dram = dram("batch_normed", (NP, D))
    t_dram = [dram(f"relation_rows_{n}", (NP * R, D)) for n in range(2)]
    lx_dram, o_dram = dram("log_rows", (NP, D)), dram("attended", (NP, D))
    msg_dram, sj_dram = dram("messages", (NP, D + H)), dram("scores", (NP, H))
    with ExitStack() as ctx:
        m = Mem(nc, ctx, "g")
        g = Shared()
        g.iota = m.sb("iota", [P, CHP])
        g.pair_start = m.sb("pair_start", [P, CHP // 2])
        g.ident = m.sb("ident", [P, P])
        g.ident_b = m.sb("ident_b", [P, P], BF16)
        g.iota_b = m.sb("iota_b", [P, P], BF16)
        g.minus_upto = m.sb("minus_upto", [P, P], BF16)
        g.ones_b = m.sb("ones_b", [P, P], BF16)
        g.ones_f = m.sb("ones_f", [P, P])
        g.rec = [m.sb(f"rec_{k}", [P, CHP, 4]) for k in range(2)]
        g.pair_tile = [m.sb(f"pair_tile_{k}", [P, CHP // 2], I32) for k in range(2)]
        make_constants(nc, g)
        g.x = m.sb("x", [P, T, D])
        g.acc = m.sb("acc", [P, T + 1, D + H])
        g.si, g.sj = m.sb("si", [P, T, H]), m.sb("sj", [P, T, H])
        g.sm = m.sb("sm", [P, T + 1, 2 * H])
        g.sm3 = m.sb("sm3", [P, T + 1, 3 * 2 * H], BF16)
        g.big = m.sb("big", [P, (T + 1) * H * P])
        g.h = g.big[:, 0:T * D].rearrange("p (t d) -> p t d", d=D)
        g.acc2 = g.big[:, T * D:T * D + (T + 1) * (D + 1)].rearrange("p (t d) -> p t d", d=D + 1)
        g.y = g.h
        g.tmp = g.big[:, T * D:2 * T * D].rearrange("p (t d) -> p t d", d=D)
        sort_edges(nc, g, a, h_dram)
        clear(nc, (g.acc[:], g.acc2))
        aggregate(nc, g, "in", 0, h_dram.ap(), D, 0, g.acc, True, 1)
        aggregate(nc, g, "out", 1, h_dram.ap(), D, 0, g.acc2, True, 1)
        gated_update(nc, g, a)
        relation_tables(nc, g, a, "mix", t_dram[0], False)
        aggregate(nc, g, "rel1", 0, t_dram[0].ap(), D, 1, g.acc, False, 0)
        relu_update(nc, g, "relu1", a["L1_gnn_bias"])
        hyperbolic_prepare(nc, g, a, lx_dram, msg_dram, sj_dram)
        neighbour_max(nc, g, sj_dram)
        clear(nc, (g.acc[:],))
        attend(nc, g, msg_dram)
        hyperbolic_finish(nc, g, a, msg_dram, o_dram)
        relation_tables(nc, g, a, "rel", t_dram[1], True)
        aggregate(nc, g, "rel3", 1, t_dram[1].ap(), D, 1, g.acc, False, 0)
        relu_update(nc, g, "relu3", a["L3_gnn_bias"], out=out)


def clear(nc, parts):
    with ExitStack() as ctx:
        block = ctx.enter_context(nc.Block())

        @block.vector
        def _(dve):
            for part in parts:
                nc.vector.memset(part, 0.0)


_TURNED = {"L0_gnn_W_in": "L0_gnn_W_in_T", "L0_gnn_W_out": "L0_gnn_W_out_T", "L2_gnn_W": "L2_gnn_W_T"}


def kernel(**inputs):
    import numpy as _np
    import concourse.bacc as _bacc
    from concourse import mybir as _mybir
    from concourse.bass_utils import run_bass_kernel_spmd as _run

    nc = _bacc.Bacc("TRN2", target_bir_lowering=False, num_devices=1)
    arrays, args = {}, {}
    for name, a in inputs.items():
        a = _np.asarray(a)
        name, a = (_TURNED[name], a.T) if name in _TURNED else (name, a)
        a = _np.ascontiguousarray(a)
        arrays[f"in_{name}"] = a
        args[name] = nc.dram_tensor(f"in_{name}", a.shape, _mybir.dt.from_np(a.dtype), kind="ExternalInput").ap()
    out = nc.dram_tensor("out_0", (N, D), F32, kind="ExternalOutput").ap()
    build(nc, args, out)
    return _run(nc, [arrays], core_ids=[0]).results[0]["out_0"]
```
